# Optimizing a Trainium2 kernel written in Bass

```python
import numpy as np
import jax
import jax.numpy as jnp

def _softmax(x, axis=-1):
    return jax.nn.softmax(x, axis=axis)

def _gelu(x):
    return jax.nn.gelu(x, approximate=True)

def _silu(x):
    return jax.nn.silu(x)

def _sigmoid(x):
    return jax.nn.sigmoid(x)

def _layernorm(x, axis=-1, eps=1e-05):
    m = jnp.mean(x, axis=axis, keepdims=True)
    v = jnp.var(x, axis=axis, keepdims=True)
    return (x - m) / jnp.sqrt(v + eps)

def _scatter_add(tgt, idx, src, axis=0):
    return tgt.at[idx].add(src)

def _segment_sum(src, seg, n):
    return jax.ops.segment_sum(src, seg, n)
kernel_name = 'mk_seq_preln_d1_jaxref_r8_549cf1'

def setup_inputs(seed: int=0):
    np.random.seed(seed)
    _w = jnp.asarray

    def _L0_attn_setup():
        import jax, jax.numpy as jnp
        import numpy as np
        EPS = 1e-05
        HEADS = 16
        DIM_HEAD = 64
        SCALE = DIM_HEAD ** (-0.5)

        def _layernorm(x, g, b):
            mu = jnp.mean(x, axis=-1, keepdims=True)
            var = jnp.var(x, axis=-1, keepdims=True)
            return (x - mu) * jax.lax.rsqrt(var + EPS) * g + b
        key = jax.random.key(seed)
        ks = jax.random.split(key, 4)
        b, n, dim = (2, 256, 128)
        inner = HEADS * DIM_HEAD
        x = jax.random.normal(ks[0], (b, n, dim), dtype=jnp.float32)
        Wq = jax.random.normal(ks[1], (dim, inner), dtype=jnp.float32) * dim ** (-0.5)
        Wkv = jax.random.normal(ks[2], (dim, 2 * DIM_HEAD), dtype=jnp.float32) * dim ** (-0.5)
        Wo = jax.random.normal(ks[3], (inner, dim), dtype=jnp.float32) * inner ** (-0.5)
        return {'x': x, 'ln1_g': jnp.ones((dim,), jnp.float32), 'ln1_b': jnp.zeros((dim,), jnp.float32), 'Wq': Wq, 'Wkv': Wkv, 'Wo': Wo, 'ln2_g': jnp.ones((dim,), jnp.float32), 'ln2_b': jnp.zeros((dim,), jnp.float32)}
    _L0_attn_in = _L0_attn_setup()

    def _L0_ffn_setup():
        import jax, jax.numpy as jnp
        import numpy as np
        H = 128
        F = 512
        E = 8
        TOP_K = 2
        B, S = (1, 256)
        key = jax.random.key(seed)
        k0, k1, k2, k3 = jax.random.split(key, 4)
        hidden_states = jax.random.normal(k0, (B, S, H), dtype=jnp.float32)
        gate_w = jax.random.normal(k1, (E, H), dtype=jnp.float32) * 0.02
        gate_up_w = jax.random.normal(k2, (E, 2 * F, H), dtype=jnp.float32) * 0.02
        down_w = jax.random.normal(k3, (E, H, F), dtype=jnp.float32) * 0.02
        return {'hidden_states': hidden_states, 'gate_w': gate_w, 'gate_up_w': gate_up_w, 'down_w': down_w}
    _L0_ffn_in = _L0_ffn_setup()
    _d = {'L0_attn_x': _L0_attn_in['x'], 'L0_attn_ln1_g': _L0_attn_in['ln1_g'], 'L0_attn_ln1_b': _L0_attn_in['ln1_b'], 'L0_attn_Wq': _L0_attn_in['Wq'], 'L0_attn_Wkv': _L0_attn_in['Wkv'], 'L0_attn_Wo': _L0_attn_in['Wo'], 'L0_attn_ln2_g': _L0_attn_in['ln2_g'], 'L0_attn_ln2_b': _L0_attn_in['ln2_b'], 'L0_ffn_gate_w': _L0_ffn_in['gate_w'], 'L0_ffn_gate_up_w': _L0_ffn_in['gate_up_w'], 'L0_ffn_down_w': _L0_ffn_in['down_w']}
    _x0 = _d['L0_attn_x']
    _d['L0_attn_x'] = jax.random.normal(jax.random.fold_in(jax.random.key(seed), 1), (4, 512, 128), dtype=_x0.dtype)
    del _x0
    return _d

def reference(L0_attn_x, L0_attn_ln1_g, L0_attn_ln1_b, L0_attn_Wq, L0_attn_Wkv, L0_attn_Wo, L0_attn_ln2_g, L0_attn_ln2_b, L0_ffn_gate_w, L0_ffn_gate_up_w, L0_ffn_down_w):

    def _L0_attn_ref(x, ln1_g, ln1_b, Wq, Wkv, Wo, ln2_g, ln2_b):
        import jax, jax.numpy as jnp
        import numpy as np
        EPS = 1e-05
        HEADS = 16
        DIM_HEAD = 64
        SCALE = DIM_HEAD ** (-0.5)

        def _layernorm(x, g, b):
            mu = jnp.mean(x, axis=-1, keepdims=True)
            var = jnp.var(x, axis=-1, keepdims=True)
            return (x - mu) * jax.lax.rsqrt(var + EPS) * g + b
        b, n, dim = x.shape
        xn = _layernorm(x, ln1_g, ln1_b)
        q = xn @ Wq
        kv = xn @ Wkv
        k, v = jnp.split(kv, 2, axis=-1)
        q = q.reshape(b, n, HEADS, DIM_HEAD).transpose(0, 2, 1, 3) * SCALE
        sim = jnp.einsum('bhid,bjd->bhij', q, k)
        attn = jax.nn.softmax(sim.astype(jnp.float32), axis=-1).astype(x.dtype)
        out = jnp.einsum('bhij,bjd->bhid', attn, v)
        out = out.transpose(0, 2, 1, 3).reshape(b, n, HEADS * DIM_HEAD)
        return _layernorm(out @ Wo, ln2_g, ln2_b)

    def _L0_ffn_ref(hidden_states, gate_w, gate_up_w, down_w):
        import jax, jax.numpy as jnp
        import numpy as np
        H = 128
        F = 512
        E = 8
        TOP_K = 2
        B, S = (1, 256)
        b, s, h = hidden_states.shape
        x = hidden_states.reshape(-1, h)
        router_logits = x @ gate_w.T
        probs = jax.nn.softmax(router_logits.astype(jnp.float32), axis=-1)
        topw, sel = jax.lax.top_k(probs, TOP_K)
        topw = topw / jnp.sum(topw, axis=-1, keepdims=True)
        topw = topw.astype(x.dtype)
        combine = jnp.sum(jax.nn.one_hot(sel, E, dtype=x.dtype) * topw[..., None], axis=1)
        gu = jnp.einsum('th,efh->etf', x, gate_up_w)
        gate, up = (gu[..., :F], gu[..., F:])
        hact = up * jax.nn.gelu(gate, approximate=False)
        expert_out = jnp.einsum('etf,ehf->eth', hact, down_w)
        out = jnp.einsum('eth,te->th', expert_out, combine)
        return out.reshape(b, s, h)
    x = L0_attn_x
    x = x + _L0_attn_ref(_layernorm(x, axis=-1), L0_attn_ln1_g, L0_attn_ln1_b, L0_attn_Wq, L0_attn_Wkv, L0_attn_Wo, L0_attn_ln2_g, L0_attn_ln2_b)
    x = x + _L0_ffn_ref(_layernorm(x, axis=-1), L0_ffn_gate_w, L0_ffn_gate_up_w, L0_ffn_down_w)
    return x

_drawn_inputs = setup_inputs


def setup_inputs(seed=0):
    import zlib

    import numpy as np

    out = dict(_drawn_inputs(seed))
    spreads = {'L0_attn_ln1_g': (1.0, 0.2),
     'L0_attn_ln1_b': (0.0, 0.1),
     'L0_attn_ln2_g': (1.0, 0.2),
     'L0_attn_ln2_b': (0.0, 0.1)}
    factors = {'L0_ffn_gate_w': 8.0, 'L0_ffn_gate_up_w': 8.0, 'L0_ffn_down_w': 8.0}
    for name, (base, spread) in spreads.items():
        noise = np.random.default_rng([zlib.crc32(name.encode()), seed]).standard_normal(out[name].shape)
        drawn = base * np.exp(spread * noise) if base else spread * noise
        out[name] = jnp.asarray(drawn.astype(out[name].dtype))
    for name, factor in factors.items():
        out[name] = (out[name] * factor).astype(out[name].dtype)
    return out
```

```python
from contextlib import ExitStack

import concourse.bass as bass
from concourse import mybir

F32 = mybir.dt.float32
F32R = mybir.dt.float32r
ALU = mybir.AluOpType
ACT = mybir.ActivationFunctionType
AX_X = mybir.AxisListType.X

P = 128
HEADS = 16
DH = 64
EPS = 1e-5
UH = 8
UP = UH // 2
JT = 4
TOP_K = 2
SUM_SLOTS = 6
RAW_SLOTS = 6


def attention_schedule(units):
    steps = [("Q", 0, p) for p in range(UP)] + [("MAX", 0, s) for s in range(2 * UH)] + [("SHIFT", 0, 0)]
    if units > 1:
        steps.append(("Q", 1, 0))
    slots = UH * JT
    for u in range(units + 1):
        for n in range(slots):
            i, jt = divmod(n, JT)
            if u < units:
                steps.append(("EXP", u, n))
            if u + 1 < units:
                for s in range(2 * UH):
                    if (3 * s) // 2 == n:
                        steps.append(("MAX", u + 1, s))
                if n in (1, 7, 13):
                    steps.append(("Q", u + 1, n // 6 + 1))
                if n == 26:
                    steps.append(("SHIFT", u + 1, 0))
            if u + 2 < units and n == 29:
                steps.append(("Q", u + 2, 0))
            if jt == 1:
                if i == 0 and u > 0:
                    steps.append(("PV", u - 1, UP - 1))
                elif i in (2, 4, 6) and u < units:
                    steps.append(("PV", u, i // 2 - 1))
            if jt == 2:
                if i == 0 and u > 0:
                    steps.append(("RAW", u - 1, UP - 1))
                elif i in (2, 4, 6) and u < units:
                    steps.append(("RAW", u, i // 2 - 1))
            if u > 0:
                if n == 7:
                    steps.append(("SUM", u - 1, 1))
                if n == 8:
                    steps.append(("RECIP", u - 1, 0))
                if jt == 3 and 3 <= i <= 6:
                    steps.append(("NORM", u - 1, i - 3))
                if jt == 3 and 4 <= i <= 7:
                    steps.append(("OUT", u - 1, i - 4))
            if u < units and n == 30:
                steps.append(("SUM", u, 0))
    return steps


def before(steps, kind):
    n, out = 0, []
    for s in steps:
        out.append(n)
        n += s[0] == kind
    return out


def bass_preln_mqa_moe_kernel(nc, x, ln1_g, ln1_b, wq, wkv, wo, ln2_g, ln2_b, gate_wT, gate_upT, downT,
                              eye, head_rows, sum_rows, lower, out):
    NB, S, D = x.shape
    T = NB * S
    TPB = S // P
    E = gate_wT.shape[1]
    F = gate_upT.shape[2] // 2
    FC = F // P
    UNITS = NB * HEADS // UH
    PAIRS = HEADS // 2
    SCALE = float(DH) ** -0.5
    assert D == P and S == 4 * P and JT == TPB and UNITS == 2 * NB

    x_t = x.rearrange("b (t p) d -> b p t d", p=P)
    out_t = out.rearrange("b (t p) d -> b p t d", p=P)
    scratch = nc.dram_tensor("combine_rows", [E, T], F32).ap()
    steps = attention_schedule(UNITS)

    with ExitStack() as whole:
        def sb(stack, name, shape, dt=F32):
            return stack.enter_context(nc.sbuf_tensor(name, shape, dt))

        def ps(stack, name, shape):
            return stack.enter_context(nc.psum_tensor(name, shape, F32))

        def sem(name):
            return whole.enter_context(nc.semaphore(name))

        ident = sb(whole, "ident", [P, P])
        yT = sb(whole, "yT", [P, T])
        stats = sb(whole, "stats", [P, TPB, 6])
        moments = sb(whole, "moments", [P, TPB, 2])
        var_eps = sb(whole, "var_eps", [P, TPB])
        rstd = sb(whole, "rstd", [P, TPB])
        minus_half = sb(whole, "minus_half", [P, TPB])

        with ExitStack() as att:
            gcol = sb(att, "gcol", [P, 1])
            bcol = sb(att, "bcol", [P, 1])
            xh = sb(att, "xh", [P, T], F32R)
            xl = sb(att, "xl", [P, T], F32R)
            khh = sb(att, "khh", [P, T], F32R)
            kly = sb(att, "kly", [P, T], F32R)
            v = sb(att, "v", [P, NB * TPB, DH])
            wqh = sb(att, "wqh", [P, HEADS * DH], F32R)
            wql = sb(att, "wql", [P, HEADS * DH], F32R)
            wkh = sb(att, "wkh", [P, P], F32R)
            wkl = sb(att, "wkl", [P, P], F32R)
            wvh = sb(att, "wvh", [P, DH], F32R)
            wvl = sb(att, "wvl", [P, DH], F32R)
            woh = sb(att, "woh", [P, PAIRS, P], F32R)
            wol = sb(att, "wol", [P, PAIRS, P], F32R)
            q_hl = sb(att, "q_hl", [P, 2, UH, S], F32R)
            q_hm = sb(att, "q_hm", [P, 2, UH, S], F32R)
            rowmax = sb(att, "rowmax", [P, 2, TPB, UH])
            mrow = sb(att, "mrow", [UH, 2, S], F32R)
            prob = sb(att, "prob", [P, 4, JT, S])
            fold = sb(att, "fold", [P, 2, S])
            psums = sb(att, "psums", [P, SUM_SLOTS, S])
            xin = fold[:, :, :].rearrange("p a (t d) -> p a t d", d=P)
            sumsel = sb(att, "sumsel", [P, 2, 32])
            headsel = sb(att, "headsel", [P, UP, P], F32R)
            rih = sb(att, "rih", [P, S], F32R)
            ril = sb(att, "ril", [P, S], F32R)
            raw = sb(att, "raw", [P, RAW_SLOTS, S])
            ao = sb(att, "ao", [P, S])
            xnT = ao
            rinv = ao
            aoh = sb(att, "aoh", [P, 2, S], F32R)
            aol = sb(att, "aol", [P, 2, S], F32R)
            wq_raw = prob[:, 0, 0:2, :].rearrange("p a s -> p (a s)")
            wo_raw = prob[:, 0, 2:4, :].rearrange("p a (c n) -> p (a c) n", n=P)
            wk_raw = prob[:, 1, 0, 0:P]
            wv_raw = prob[:, 1, 0, P:P + DH]
            hs_raw = prob[:, 1, 1, :].rearrange("p (u n) -> p u n", n=P)

            q_ps = ps(att, "q_ps", [P, S])
            max_ps = ps(att, "max_ps", [P, 2, S])
            s_ps = ps(att, "s_ps", [P, 2, S])
            pv_ps = ps(att, "pv_ps", [P, S])
            sum_ps = ps(att, "sum_ps", [P, S])
            y_ps = ps(att, "y_ps", [P, S])

            names = """consts_in wkv_in wq_in wo_in ones_set half_set wkv_split wq_split wo_split headsel_set
                ln_stats ln_rstd dve_own pool_own xn_ready xnT_ps xnT_sb xh_ready xl_ready kv_ps kh_ready
                kv_ready q_mm q_hi q_lo q_top max_mm max_done shift_mm mrow_ready score_mm exp_done
                pv_mm raw_ready prob_folded head_sum sum_mm recip_done norm_mm ao_ready aoh_ready ao_split
                out_mm y_ready""".split()
            (consts_in, wkv_in, wq_in, wo_in, ones_set, half_set, wkv_split, wq_split, wo_split, headsel_set,
             ln_stats, ln_rstd, dve_own, pool_own, xn_ready, xnT_ps, xnT_sb, xh_ready, xl_ready, kv_ps,
             kh_ready, kv_ready, q_mm, q_hi, q_lo, q_top, max_mm, max_done, shift_mm, mrow_ready,
             score_mm, exp_done, pv_mm, raw_ready, prob_folded, head_sum, sum_mm, recip_done, norm_mm, ao_ready,
             aoh_ready, ao_split, out_mm, y_ready) = [sem(n) for n in names]
            x_in = [sem(f"x_in{n}") for n in range(2)]
            mrow_in = [sem(f"mrow_in{n}") for n in range(2)]

            block = att.enter_context(nc.Block())

            @block.sync
            def _(sp):
                sp.dma_start(xin[:, 0], x_t[0]).then_inc(x_in[0], 16)
                for dst, src in ((ident[:, :], eye), (gcol[:, :], ln1_g.rearrange("(p o) -> p o", o=1)),
                                 (bcol[:, :], ln1_b.rearrange("(p o) -> p o", o=1)),
                                 (hs_raw, head_rows), (sumsel[:, :, :], sum_rows)):
                    sp.dma_start(dst, src).then_inc(consts_in, 16)
                sp.dma_start(wk_raw[:, 0:DH], wkv[:, 0:DH]).then_inc(wkv_in, 16)
                sp.dma_start(wk_raw[:, DH:P], wkv[:, 0:DH]).then_inc(wkv_in, 16)
                sp.dma_start(wv_raw, wkv[:, DH:2 * DH]).then_inc(wkv_in, 16)
                sp.dma_start(wq_raw, wq).then_inc(wq_in, 16)
                sp.dma_start(wo_raw, wo.rearrange("(c p) n -> p c n", p=P)).then_inc(wo_in, 16)
                for b in range(1, NB):
                    if b >= 2:
                        sp.wait_ge(xnT_ps, b - 1)
                    sp.dma_start(xin[:, b % 2], x_t[b]).then_inc(x_in[b % 2], 16)
                for kind, u, _ in steps:
                    if kind == "SHIFT":
                        sp.wait_ge(mrow_ready, 2 * (u + 1))
                        if u >= 2:
                            sp.wait_ge(score_mm, (u - 1) * UH * JT)
                        for part in range(2):
                            sp.dma_start(q_hm[DH + part:DH + part + 1, u % 2, :, :].bitcast(F32),
                                         mrow[:, part, :].bitcast(F32)).then_inc(mrow_in[u % 2], 16)

            @block.gpsimd
            def _(pool):
                own = 0
                nc.gpsimd.memset(minus_half[:, :], -0.5).then_inc(half_set, 1)
                pool.wait_ge(half_set, 1)

                def split(raw_ap, high, low, done):
                    nonlocal own
                    nc.gpsimd.tensor_scalar(high, raw_ap, 1.0, 1.0, ALU.mult, ALU.mult).then_inc(pool_own, 1)
                    own += 1
                    pool.wait_ge(pool_own, own)
                    nc.gpsimd.tensor_tensor(low, raw_ap, high.bitcast(F32), ALU.subtract).then_inc(done, 1)

                def rsqrt(n):
                    nonlocal own
                    pool.wait_ge(ln_stats, n + 1)
                    nc.gpsimd.tensor_scalar(var_eps[:, :], moments[:, :, 1], 1.0, EPS, ALU.mult,
                                            ALU.add).then_inc(pool_own, 1)
                    own += 1
                    pool.wait_ge(pool_own, own)
                    nc.gpsimd.tensor_tensor(rstd[:, :], var_eps[:, :], minus_half[:, :],
                                            ALU.pow).then_inc(ln_rstd, 1)

                rsqrt(0)
                rsqrt(1)
                pool.wait_ge(wkv_in, 48)
                split(wk_raw, wkh[:, :], wkl[:, :], wkv_split)
                split(wv_raw, wvh[:, :], wvl[:, :], wkv_split)
                rsqrt(2)
                rsqrt(3)
                pool.wait_ge(wq_in, 16)
                split(wq_raw[:, 0:S], wqh[:, 0:S], wql[:, 0:S], wq_split)
                rsqrt(4)
                rsqrt(5)
                split(wq_raw[:, S:2 * S], wqh[:, S:2 * S], wql[:, S:2 * S], wq_split)
                rsqrt(6)
                rsqrt(7)
                pool.wait_ge(consts_in, 80)
                nc.gpsimd.tensor_scalar(headsel[:, :, :], hs_raw, 1.0, 1.0, ALU.mult,
                                        ALU.mult).then_inc(headsel_set, 1)
                pool.wait_ge(wo_in, 16)
                split(wo_raw, woh[:, :, :], wol[:, :, :], wo_split)

                for kind, u, a in steps:
                    if kind == "Q":
                        k = u * UP + a
                        pool.wait_ge(q_hi, 2 * (k + 1))
                        pair = slice(2 * a, 2 * a + 2)
                        nc.gpsimd.tensor_scalar(q_hm[0:DH, u % 2, pair, :], q_hl[0:DH, u % 2, pair, :].bitcast(F32),
                                                1.0, 1.0, ALU.mult, ALU.mult).then_inc(q_top, 1)
                    if kind == "EXP" and a % JT == JT - 1:
                        head = u * UH + a // JT
                        pool.wait_ge(exp_done, (head + 1) * JT)
                        if head >= 1:
                            pool.wait_ge(head_sum, head)
                        nc.gpsimd.tensor_tensor(fold[:, :, :], prob[:, head % 4, 0:2, :], prob[:, head % 4, 2:4, :],
                                                ALU.add).then_inc(prob_folded, 1)
                        pool.wait_ge(prob_folded, head + 1)
                        if head >= SUM_SLOTS:
                            pool.wait_ge(sum_mm, (head - SUM_SLOTS) // 4 + 1)
                        nc.gpsimd.tensor_tensor(psums[:, head % SUM_SLOTS, :], fold[:, 0, :], fold[:, 1, :],
                                                ALU.add).then_inc(head_sum, 1)

            @block.vector
            def _(dve):
                own = 0

                def link(ins):
                    nonlocal own
                    ins.then_inc(dve_own, 1)
                    own += 1
                    dve.wait_ge(dve_own, own)

                def layer_norm(n, tile):
                    for t in range(TPB):
                        last = nc.vector.bn_stats(stats[:, t, :], tile[:, t, :])
                    link(last)
                    for t in range(TPB):
                        last = nc.vector.bn_aggr(moments[:, t, :], stats[:, t, :])
                    last.then_inc(ln_stats, 1)
                    dve.wait_ge(ln_rstd, n + 1)
                    for t in range(TPB):
                        last = nc.vector.tensor_scalar(tile[:, t, :], tile[:, t, :], moments[:, t, 0:1],
                                                       rstd[:, t:t + 1], ALU.subtract, ALU.mult)
                    return last

                def normalise(b):
                    dve.wait_ge(x_in[b % 2], 16 * (b // 2 + 1))
                    link(layer_norm(2 * b, xin[:, b % 2]))
                    layer_norm(2 * b + 1, xin[:, b % 2]).then_inc(xn_ready, 1)

                def scale_and_split(b):
                    dve.wait_ge(xnT_ps, b + 1)
                    if b == 0:
                        dve.wait_ge(consts_in, 80)
                    else:
                        dve.wait_ge(xh_ready, b)
                    nc.vector.tensor_scalar(xnT[:, :], q_ps[:, :], gcol[:, :], bcol[:, :], ALU.mult,
                                            ALU.add).then_inc(xnT_sb, 1)
                    dve.wait_ge(xh_ready, b + 1)
                    dve.wait_ge(xnT_sb, b + 1)
                    cols = slice(b * S, (b + 1) * S)
                    nc.vector.tensor_tensor(xl[:, cols], xnT[:, :], xh[:, cols].bitcast(F32),
                                            ALU.subtract).then_inc(xl_ready, 1)

                def split_kv(b):
                    dve.wait_ge(kv_ps, b + 1)
                    nc.vector.tensor_copy(v[:, b * TPB:(b + 1) * TPB, :],
                                          y_ps[:, 0:TPB * DH].rearrange("p (t d) -> p t d", d=DH))
                    dve.wait_ge(kh_ready, b + 1)
                    cols = slice(b * S, (b + 1) * S)
                    nc.vector.tensor_tensor(kly[0:DH, cols], pv_ps[0:DH, :], khh[0:DH, cols].bitcast(F32),
                                            ALU.subtract).then_inc(kv_ready, 1)

                nc.vector.memset(kly[DH:DH + 2, :].bitcast(F32), 1.0).then_inc(ones_set, 1)
                for b in range(NB):
                    normalise(b)
                    scale_and_split(b)
                    if b > 0:
                        split_kv(b - 1)
                split_kv(NB - 1)

                for kind, u, a in steps:
                    if kind == "Q":
                        for hd in range(2):
                            h = 2 * (u * UP + a) + hd
                            dve.wait_ge(q_hi, h + 1)
                            nc.vector.tensor_tensor(q_hl[DH:P, u % 2, 2 * a + hd, :], q_ps[DH * hd:DH * hd + DH, :],
                                                    q_hl[0:DH, u % 2, 2 * a + hd, :].bitcast(F32),
                                                    ALU.subtract).then_inc(q_lo, 1)
                    if kind == "MAX":
                        i, half = divmod(a, 2)
                        dve.wait_ge(max_mm, u * 2 * UH + a + 1)
                        if a == 0 and u >= 2:
                            dve.wait_ge(shift_mm, u - 1)
                        nc.vector.tensor_reduce(rowmax[:, u % 2, 2 * half:2 * half + 2, i], max_ps[:, :, :], AX_X,
                                                ALU.max).then_inc(max_done, 1)
                    if kind == "SHIFT":
                        dve.wait_ge(shift_mm, u + 1)
                        if u >= 1:
                            dve.wait_ge(mrow_in[(u - 1) % 2], 32 * ((u - 1) // 2 + 1))
                        nc.vector.tensor_scalar(mrow[:, 0, :], q_ps[0:UH, :], -1.0, None,
                                                ALU.mult).then_inc(mrow_ready, 1)
                        dve.wait_ge(mrow_ready, 2 * u + 1)
                        nc.vector.scalar_tensor_tensor(out=mrow[:, 1, :], in0=q_ps[0:UH, :], scalar=-1.0,
                                                       in1=mrow[:, 0, :].bitcast(F32), op0=ALU.mult,
                                                       op1=ALU.subtract).then_inc(mrow_ready, 1)
                    if kind == "RECIP":
                        dve.wait_ge(sum_mm, 2 * (u + 1))
                        link(nc.vector.reciprocal(rinv[:, :], sum_ps[:, :]))
                        if u >= 1:
                            dve.wait_ge(norm_mm, u * UP)
                        link(nc.vector.tensor_copy(rih[:, :], rinv[:, :]))
                        nc.vector.tensor_tensor(ril[:, :], rinv[:, :], rih[:, :].bitcast(F32),
                                                ALU.subtract).then_inc(recip_done, 1)
                    if kind == "NORM":
                        k = u * UP + a
                        dve.wait_ge(norm_mm, k + 1)
                        dve.wait_ge(raw_ready, k + 1)
                        if k >= 1:
                            dve.wait_ge(ao_split, k)
                        nc.vector.tensor_tensor(ao[:, :], sum_ps[:, :], raw[:, k % RAW_SLOTS, :],
                                                ALU.mult).then_inc(ao_ready, 1)
                    if kind == "NORM":
                        k = u * UP + a
                        dve.wait_ge(aoh_ready, k + 1)
                        nc.vector.tensor_tensor(aol[:, k % 2, :], ao[:, :], aoh[:, k % 2, :].bitcast(F32),
                                                ALU.subtract).then_inc(ao_split, 1)

            @block.scalar
            def _(act):
                for b in range(NB):
                    cols = slice(b * S, (b + 1) * S)
                    act.wait_ge(xnT_sb, b + 1)
                    nc.scalar.activation(xh[:, cols], xnT[:, :], ACT.Copy).then_inc(xh_ready, 1)
                    act.wait_ge(kv_ps, b + 1)
                    nc.scalar.activation(khh[:, cols], pv_ps[:, :], ACT.Copy).then_inc(kh_ready, 1)

                for kind, u, a in steps:
                    if kind == "Q":
                        act.wait_ge(q_mm, u * UP + a + 1)
                        if u >= 2:
                            act.wait_ge(score_mm, ((u - 2) * UH + 2 * a + 2) * JT)
                        for hd in range(2):
                            nc.scalar.activation(q_hl[0:DH, u % 2, 2 * a + hd, :], q_ps[DH * hd:DH * hd + DH, :],
                                                 ACT.Copy).then_inc(q_hi, 1)
                    if kind == "EXP":
                        k = u * UH * JT + a
                        head, jt = divmod(k, JT)
                        act.wait_ge(score_mm, k + 1)
                        if head < 4 and jt == 0:
                            if head == 0:
                                act.wait_ge(wkv_split, 2)
                                act.wait_ge(wq_split, 2)
                                act.wait_ge(headsel_set, 1)
                                act.wait_ge(wo_split, 1)
                        elif jt == 0:
                            act.wait_ge(pv_mm, (head - 4) // 2 + 1)
                            act.wait_ge(prob_folded, head - 3)
                        nc.scalar.activation(prob[:, head % 4, jt, :], s_ps[:, k % 2, :], ACT.Exp,
                                             scale=SCALE).then_inc(exp_done, 1)
                    if kind == "RAW":
                        k = u * UP + a
                        act.wait_ge(pv_mm, k + 1)
                        if k >= RAW_SLOTS:
                            act.wait_ge(ao_ready, k - RAW_SLOTS + 1)
                        nc.scalar.activation(raw[:, k % RAW_SLOTS, :], pv_ps[:, :], ACT.Copy).then_inc(raw_ready, 1)
                    if kind == "NORM":
                        k = u * UP + a
                        act.wait_ge(ao_ready, k + 1)
                        if k >= 2:
                            act.wait_ge(out_mm, k - 1)
                        nc.scalar.activation(aoh[:, k % 2, :], ao[:, :], ACT.Copy).then_inc(aoh_ready, 1)
                    if kind == "OUT" and (u * UP + a) % PAIRS == PAIRS - 1:
                        b = (u * UP + a) // PAIRS
                        act.wait_ge(out_mm, PAIRS * (b + 1))
                        nc.scalar.activation(yT[:, b * S:(b + 1) * S], y_ps[:, :], ACT.Copy).then_inc(y_ready, 1)

            @block.tensor
            def _(pe):
                def product(dst, wh, wl, mh, ml, start, stop):
                    nc.tensor.matmul(dst, wh, mh, start=start, stop=False, skip_group_check=True)
                    nc.tensor.matmul(dst, wl, mh, start=False, stop=False, skip_group_check=True)
                    return nc.tensor.matmul(dst, wh, ml, start=False, stop=stop, skip_group_check=True)

                pe.wait_ge(consts_in, 80)
                for b in range(NB):
                    cols = slice(b * S, (b + 1) * S)
                    pe.wait_ge(xn_ready, b + 1)
                    if b >= 1:
                        pe.wait_ge(xnT_sb, b)
                    for t in range(TPB):
                        last = nc.tensor.transpose(q_ps[:, t * P:(t + 1) * P], xin[:, b % 2, t, :], ident[:, :])
                    last.then_inc(xnT_ps, 1)
                    pe.wait_ge(xl_ready, b + 1)
                    if b == 0:
                        pe.wait_ge(wkv_split, 2)
                    else:
                        pe.wait_ge(kv_ready, b)
                    product(pv_ps[:, :], wkh[:, :], wkl[:, :], xh[:, cols], xl[:, cols], True, True)
                    for t in range(TPB):
                        tile = slice(b * S + t * P, b * S + (t + 1) * P)
                        last = product(y_ps[:, t * DH:(t + 1) * DH], xh[:, tile], xl[:, tile], wvh[:, :],
                                       wvl[:, :], t == 0, t == TPB - 1)
                    last.then_inc(kv_ps, 1)
                pe.wait_ge(kv_ready, NB)
                pe.wait_ge(wq_split, 2)

                shifts_before = before(steps, "SHIFT")
                for n, (kind, u, a) in enumerate(steps):
                    b = u // 2
                    cols = slice(b * S, (b + 1) * S)
                    if kind == "Q":
                        k = u * UP + a
                        c = k % PAIRS
                        if k >= 1:
                            pe.wait_ge(q_lo, 2 * k)
                        if shifts_before[n]:
                            pe.wait_ge(mrow_ready, 2 * shifts_before[n])
                        wcols = slice(c * P, (c + 1) * P)
                        product(q_ps[:, :], wqh[:, wcols], wql[:, wcols], xh[:, cols], xl[:, cols],
                                True, True).then_inc(q_mm, 1)
                    if kind == "MAX":
                        i, half = divmod(a, 2)
                        k = u * 2 * UH + a
                        pe.wait_ge(q_lo, u * UH + i + 1)
                        if k >= 1:
                            pe.wait_ge(max_done, k)
                        for w in range(2):
                            it = 2 * half + w
                            last = nc.tensor.matmul(max_ps[:, w, :], q_hl[:, u % 2, i, it * P:(it + 1) * P],
                                                    khh[:, cols], start=True, stop=True)
                        last.then_inc(max_mm, 1)
                    if kind == "SHIFT":
                        pe.wait_ge(max_done, (u + 1) * 2 * UH)
                        pe.wait_ge(q_lo, (u + 1) * UH)
                        for t in range(TPB):
                            last = nc.tensor.transpose(q_ps[0:UH, t * P:(t + 1) * P], rowmax[:, u % 2, t, :],
                                                       ident[:, :])
                        last.then_inc(shift_mm, 1)
                    if kind == "EXP":
                        k = u * UH * JT + a
                        i, jt = divmod(a, JT)
                        if a == 0:
                            if u == 0:
                                pe.wait_ge(ones_set, 1)
                            pe.wait_ge(mrow_in[u % 2], 32 * (u // 2 + 1))
                        if a % (2 * JT) == 0:
                            pe.wait_ge(q_top, u * UP + i // 2 + 1)
                        if k >= 2:
                            pe.wait_ge(exp_done, k - 1)
                        keys = slice(b * S + jt * P, b * S + (jt + 1) * P)
                        nc.tensor.matmul(s_ps[:, k % 2, :], khh[:, keys], q_hl[:, u % 2, i, :],
                                         start=True, stop=False)
                        nc.tensor.matmul(s_ps[:, k % 2, :], kly[0:DH + 2, keys], q_hm[0:DH + 2, u % 2, i, :],
                                         start=False, stop=True).then_inc(score_mm, 1)
                    if kind == "PV":
                        k = u * UP + a
                        pe.wait_ge(exp_done, (k + 1) * 2 * JT)
                        if k >= 1:
                            pe.wait_ge(raw_ready, k)
                        for jt in range(JT):
                            for hd in range(2):
                                head = 2 * k + hd
                                last = nc.tensor.matmul(pv_ps[DH * hd:DH * hd + DH, :], v[:, b * TPB + jt, :],
                                                        prob[:, head % 4, jt, :], start=(jt == 0),
                                                        stop=(jt == JT - 1))
                        last.then_inc(pv_mm, 1)
                    if kind == "SUM":
                        k = 2 * u + a
                        pe.wait_ge(head_sum, 4 * (k + 1))
                        if a == 0 and u >= 1:
                            pe.wait_ge(ao_ready, u * UP)
                        for i in range(4):
                            last = nc.tensor.matmul(sum_ps[32 * i:32 * i + 32, :], sumsel[:, a, :],
                                                    psums[:, (4 * k + i) % SUM_SLOTS, :], start=(a == 0), stop=(a == 1),
                                                    skip_group_check=True)
                        last.then_inc(sum_mm, 1)
                    if kind == "NORM":
                        k = u * UP + a
                        pe.wait_ge(recip_done, u + 1)
                        if k >= 1:
                            pe.wait_ge(ao_ready, k)
                        if k == 0:
                            pe.wait_ge(headsel_set, 1)
                        nc.tensor.matmul(sum_ps[:, :], headsel[:, a, :], rih[:, :], start=True, stop=False)
                        nc.tensor.matmul(sum_ps[:, :], headsel[:, a, :], ril[:, :], start=False,
                                         stop=True).then_inc(norm_mm, 1)
                    if kind == "OUT":
                        k = u * UP + a
                        c = k % PAIRS
                        pe.wait_ge(ao_split, k + 1)
                        if k == 0:
                            pe.wait_ge(wo_split, 1)
                        if c == 0 and b >= 1:
                            pe.wait_ge(y_ready, b)
                        product(y_ps[:, :], woh[:, c, :], wol[:, c, :], aoh[:, k % 2, :], aol[:, k % 2, :],
                                c == 0, c == PAIRS - 1).then_inc(out_mm, 1)

        LN_DONE = 2 * NB
        with ExitStack() as moe:
            x1 = sb(moe, "x1", [P, NB * TPB, P])
            g2 = sb(moe, "g2", [P, P])
            b2 = sb(moe, "b2", [P, P])
            z = sb(moe, "z", [P, TPB, P])
            x3 = sb(moe, "x3", [P, TPB, P])
            x3T = sb(moe, "x3T", [P, T])
            x3h = sb(moe, "x3h", [P, T], F32R)
            x3l = sb(moe, "x3l", [P, T], F32R)
            gw = sb(moe, "gw", [P, E])
            tri = sb(moe, "tri", [P, E, E])
            r1 = sb(moe, "r1", [P, TPB])
            r2 = sb(moe, "r2", [P, TPB])
            pr = sb(moe, "pr", [P, TPB, E])
            cmp = sb(moe, "cmp", [P, TPB, E, E])
            eqs = sb(moe, "eqs", [P, TPB, E, E])
            cnt = sb(moe, "cnt", [P, TPB, E])
            comb = sb(moe, "comb", [P, TPB, E])
            combT = sb(moe, "combT", [E, 2, S])
            wgu_raw = sb(moe, "wgu_raw", [P, 2, 2 * F])
            wdn_raw = sb(moe, "wdn_raw", [P, 2, FC, P])
            wguh = sb(moe, "wguh", [P, 2, 2 * F], F32R)
            wgul = sb(moe, "wgul", [P, 2, 2 * F], F32R)
            wdnh = sb(moe, "wdnh", [P, 2, FC, P], F32R)
            wdnl = sb(moe, "wdnl", [P, 2, FC, P], F32R)
            cb = sb(moe, "cb", [P, 4, S])
            xe = sb(moe, "xe", [P, S])
            xeh = sb(moe, "xeh", [P, 2, S], F32R)
            xel = sb(moe, "xel", [P, 2, S], F32R)
            gl = sb(moe, "gl", [P, 2, S])
            ha = sb(moe, "ha", [P, 2, S])
            hh = sb(moe, "hh", [P, 4, S], F32R)
            hl = sb(moe, "hl", [P, 4, S], F32R)
            acc = sb(moe, "acc", [P, T])

            gate_ps = ps(moe, "gate_ps", [P, 2, S])
            up_ps = ps(moe, "up_ps", [P, 2, S])
            down_ps = ps(moe, "down_ps", [P, 2, S])
            tr_ps = ps(moe, "tr_ps", [P, S])
            ro_ps = ps(moe, "ro_ps", [P, S])

            names = """consts2_in yT_tr z_ready x3_ready x3_tr x3T_ready x3h_ready x3l_ready
                logit_mm logit_max prob_exp comb_ready comb_tr combT_ready w_free w_split xe_ready
                xeh_ready xel_ready gate_mm up_mm gelu_done ha_ready hh_ready hl_ready down_mm acc_done
                acc_tr out_ready out_sent pool2_own""".split()
            (consts2_in, yT_tr, z_ready, x3_ready, x3_tr, x3T_ready, x3h_ready,
             x3l_ready, logit_mm, logit_max, prob_exp, comb_ready, comb_tr, combT_ready, w_free, w_split,
             xe_ready, xeh_ready, xel_ready, gate_mm, up_mm, gelu_done, ha_ready, hh_ready, hl_ready, down_mm,
             acc_done, acc_tr, out_ready, out_sent, pool2_own) = [sem(n) for n in names]
            dve2_own = sem("dve2_own")
            x1_in = [sem(f"x1_in{n}") for n in range(NB)]
            gu_in = [sem(f"gu_in{n}") for n in range(2)]
            dn_in = [sem(f"dn_in{n}") for n in range(2)]
            cb_in = [sem(f"cb_in{n}") for n in range(4)]
            rows_out = [sem(f"rows_out{n}") for n in range(NB)]
            GROUPS = NB

            block2 = moe.enter_context(nc.Block())

            @block2.sync
            def _(sp):
                sp.dma_start(x1[:, 0:TPB, :], x_t[0]).then_inc(x1_in[0], 16)
                for dst, src in ((g2[:, :], ln2_g.partition_broadcast(P)), (b2[:, :], ln2_b.partition_broadcast(P)),
                                 (gw[:, :], gate_wT), (tri[:, :, :], lower)):
                    sp.dma_start(dst, src).then_inc(consts2_in, 16)

                def weights(e):
                    if e >= 2:
                        sp.wait_ge(w_split, 2 * (e - 1))
                    sp.dma_start(wgu_raw[:, e % 2, :], gate_upT[e]).then_inc(gu_in[e % 2], 16)
                    sp.dma_start(wdn_raw[:, e % 2, :, :],
                                 downT[e].rearrange("(c p) n -> p c n", p=P)).then_inc(dn_in[e % 2], 16)

                weights(0)
                for b in range(1, NB):
                    sp.dma_start(x1[:, b * TPB:(b + 1) * TPB, :], x_t[b]).then_inc(x1_in[b], 16)
                weights(1)
                for b in range(NB):
                    sp.wait_ge(combT_ready, b + 1)
                    sp.dma_start(scratch[:, b * S:(b + 1) * S], combT[:, b % 2, :]).then_inc(rows_out[b], 16)
                for e in range(E):
                    if e + 1 < E and e >= 1:
                        weights(e + 1)
                    for g in range(GROUPS):
                        k = e * GROUPS + g
                        if e == 0:
                            sp.wait_ge(rows_out[g], 16)
                        if k >= 4:
                            sp.wait_ge(xe_ready, k - 3)
                        sp.dma_start(cb[:, k % 4, :],
                                     scratch[e, g * S:(g + 1) * S].partition_broadcast(P)).then_inc(cb_in[k % 4], 16)
                for b in range(NB):
                    sp.wait_ge(out_ready, b + 1)
                    sp.dma_start(out_t[b], x1[:, b * TPB:(b + 1) * TPB, :]).then_inc(out_sent, 16)
                sp.wait_ge(out_sent, 16 * NB)

            @block2.gpsimd
            def _(pool):
                own = 0

                def rsqrt(n):
                    nonlocal own
                    pool.wait_ge(ln_stats, LN_DONE + n + 1)
                    nc.gpsimd.tensor_scalar(var_eps[:, :], moments[:, :, 1], 1.0, EPS, ALU.mult,
                                            ALU.add).then_inc(pool2_own, 1)
                    own += 1
                    pool.wait_ge(pool2_own, own)
                    nc.gpsimd.tensor_tensor(rstd[:, :], var_eps[:, :], minus_half[:, :],
                                            ALU.pow).then_inc(ln_rstd, 1)

                def split_weights(e):
                    nonlocal own
                    for raw_in, raw_ap, high, low in (
                            (gu_in, wgu_raw[:, e % 2, :], wguh[:, e % 2, :], wgul[:, e % 2, :]),
                            (dn_in, wdn_raw[:, e % 2, :, :], wdnh[:, e % 2, :, :], wdnl[:, e % 2, :, :])):
                        pool.wait_ge(raw_in[e % 2], 16 * (e // 2 + 1))
                        if e >= 2:
                            pool.wait_ge(down_mm, (e - 1) * GROUPS)
                        nc.gpsimd.tensor_scalar(high, raw_ap, 1.0, 1.0, ALU.mult, ALU.mult).then_inc(pool2_own, 1)
                        own += 1
                        pool.wait_ge(pool2_own, own)
                        nc.gpsimd.tensor_tensor(low, raw_ap, high.bitcast(F32), ALU.subtract).then_inc(w_split, 1)

                rsqrt(0)
                rsqrt(1)
                split_weights(0)
                for n in range(2, 2 * NB):
                    rsqrt(n)
                for e in range(E):
                    for g in range(GROUPS):
                        k = e * GROUPS + g
                        pool.wait_ge(xe_ready, k + 1)
                        if k >= 2:
                            pool.wait_ge(up_mm, (k - 1) * FC)
                        nc.gpsimd.tensor_scalar(xeh[:, k % 2, :], xe[:, :], 1.0, 1.0, ALU.mult,
                                                ALU.mult).then_inc(xeh_ready, 1)
                        if g == 0 and e + 1 < E:
                            split_weights(e + 1)

            @block2.vector
            def _(dve):
                own = 0

                def link(ins):
                    nonlocal own
                    ins.then_inc(dve2_own, 1)
                    own += 1
                    dve.wait_ge(dve2_own, own)

                def layer_norm(n, dst, src):
                    for t in range(TPB):
                        last = nc.vector.bn_stats(stats[:, t, :], src[:, t, :])
                    link(last)
                    for t in range(TPB):
                        last = nc.vector.bn_aggr(moments[:, t, :], stats[:, t, :])
                    last.then_inc(ln_stats, 1)
                    dve.wait_ge(ln_rstd, LN_DONE + n + 1)
                    for t in range(TPB):
                        last = nc.vector.tensor_scalar(dst[:, t, :], src[:, t, :], moments[:, t, 0:1],
                                                       rstd[:, t:t + 1], ALU.subtract, ALU.mult)
                    return last

                def residual(b):
                    dve.wait_ge(yT_tr, b + 1)
                    link(layer_norm(2 * b, z, tr_ps[:, :].rearrange("p (t d) -> p t d", d=P)))
                    if b == 0:
                        dve.wait_ge(consts2_in, 64)
                    link(nc.vector.tensor_tensor(z[:, :, :], z[:, :, :],
                                                 g2[:, :].unsqueeze(1).broadcast_to([P, TPB, P]), ALU.mult))
                    link(nc.vector.tensor_tensor(z[:, :, :], z[:, :, :],
                                                 b2[:, :].unsqueeze(1).broadcast_to([P, TPB, P]), ALU.add))
                    tiles = x1[:, b * TPB:(b + 1) * TPB, :]
                    dve.wait_ge(x1_in[b], 16)
                    link(nc.vector.tensor_tensor(tiles, tiles, z[:, :, :], ALU.add))
                    if b >= 1:
                        dve.wait_ge(x3_tr, b)
                    layer_norm(2 * b + 1, x3, tiles).then_inc(x3_ready, 1)

                def split_x3(b):
                    cols = slice(b * S, (b + 1) * S)
                    dve.wait_ge(x3h_ready, b + 1)
                    nc.vector.tensor_tensor(x3l[:, cols], x3T[:, cols], x3h[:, cols].bitcast(F32),
                                            ALU.subtract).then_inc(x3l_ready, 1)

                def route(b):
                    logits = ro_ps[:, 0:TPB * E].rearrange("p (t e) -> p t e", e=E)
                    dve.wait_ge(logit_mm, b + 1)
                    link(nc.vector.tensor_reduce(r1[:, :], logits, AX_X, ALU.max))
                    nc.vector.tensor_tensor(pr[:, :, :], logits, r1[:, :].unsqueeze(2).broadcast_to([P, TPB, E]),
                                            ALU.subtract).then_inc(logit_max, 1)
                    dve.wait_ge(prob_exp, b + 1)
                    link(nc.vector.tensor_reduce(r1[:, :], pr[:, :, :], AX_X, ALU.add))
                    link(nc.vector.reciprocal(r2[:, :], r1[:, :]))
                    link(nc.vector.tensor_tensor(pr[:, :, :], pr[:, :, :],
                                                 r2[:, :].unsqueeze(2).broadcast_to([P, TPB, E]), ALU.mult))
                    for t in range(TPB):
                        other = pr[:, t, :].unsqueeze(1).broadcast_to([P, E, E])
                        this = pr[:, t, :].unsqueeze(2).broadcast_to([P, E, E])
                        nc.vector.tensor_tensor(cmp[:, t], other, this, ALU.is_gt)
                        last = nc.vector.tensor_tensor(eqs[:, t], other, this, ALU.is_equal)
                    link(last)
                    link(nc.vector.tensor_tensor(eqs[:, :, :, :], eqs[:, :, :, :],
                                                 tri[:, :, :].unsqueeze(1).broadcast_to([P, TPB, E, E]), ALU.mult))
                    link(nc.vector.tensor_tensor(cmp[:, :, :, :], cmp[:, :, :, :], eqs[:, :, :, :], ALU.add))
                    link(nc.vector.tensor_reduce(cnt[:, :, :], cmp[:, :, :, :], AX_X, ALU.add))
                    link(nc.vector.tensor_scalar(cnt[:, :, :], cnt[:, :, :], TOP_K - 0.5, None, ALU.is_lt))
                    link(nc.vector.tensor_tensor(pr[:, :, :], pr[:, :, :], cnt[:, :, :], ALU.mult))
                    link(nc.vector.tensor_reduce(r1[:, :], pr[:, :, :], AX_X, ALU.add))
                    link(nc.vector.reciprocal(r2[:, :], r1[:, :]))
                    if b >= 1:
                        dve.wait_ge(comb_tr, b)
                    nc.vector.tensor_tensor(comb[:, :, :], pr[:, :, :],
                                            r2[:, :].unsqueeze(2).broadcast_to([P, TPB, E]),
                                            ALU.mult).then_inc(comb_ready, 1)

                for b in range(NB):
                    residual(b)
                    split_x3(b)
                    route(b)

                def scale_x(e, g):
                    k = e * GROUPS + g
                    dve.wait_ge(cb_in[k % 4], 16 * (k // 4 + 1))
                    if k >= 1:
                        dve.wait_ge(xeh_ready, k)
                        dve.wait_ge(xel_ready, k)
                    nc.vector.tensor_tensor(xe[:, :], x3T[:, g * S:(g + 1) * S], cb[:, k % 4, :],
                                            ALU.mult).then_inc(xe_ready, 1)
                    dve.wait_ge(xe_ready, k + 1)
                    dve.wait_ge(xeh_ready, k + 1)
                    if k >= 2:
                        dve.wait_ge(up_mm, (k - 1) * FC)
                    nc.vector.tensor_tensor(xel[:, k % 2, :], xe[:, :], xeh[:, k % 2, :].bitcast(F32),
                                            ALU.subtract).then_inc(xel_ready, 1)

                def accumulate(k):
                    e, g = divmod(k, GROUPS)
                    cols = slice(g * S, (g + 1) * S)
                    dve.wait_ge(down_mm, k + 1)
                    if e == 0:
                        nc.vector.tensor_copy(acc[:, cols], down_ps[:, k % 2, :]).then_inc(acc_done, 1)
                    else:
                        dve.wait_ge(acc_done, k - GROUPS + 1)
                        nc.vector.tensor_tensor(acc[:, cols], acc[:, cols], down_ps[:, k % 2, :],
                                                ALU.add).then_inc(acc_done, 1)

                scale_x(0, 0)
                for k in range(E * GROUPS):
                    for fc in range(FC):
                        n = k * FC + fc
                        dve.wait_ge(gelu_done, n + 1)
                        dve.wait_ge(up_mm, n + 1)
                        if n >= 2:
                            dve.wait_ge(hl_ready, n - 1)
                            dve.wait_ge(hh_ready, n - 1)
                        nc.vector.tensor_tensor(ha[:, n % 2, :], up_ps[:, n % 2, :], gl[:, n % 2, :],
                                                ALU.mult).then_inc(ha_ready, 1)
                        if fc == 0 and k + 1 < E * GROUPS:
                            scale_x(*divmod(k + 1, GROUPS))
                        if fc == 2 and k >= 1:
                            accumulate(k - 1)
                        dve.wait_ge(hh_ready, n + 1)
                        if n >= 4:
                            dve.wait_ge(down_mm, (n - 4) // FC + 1 if (n - 4) % FC == FC - 1 else (n - 4) // FC)
                        nc.vector.tensor_tensor(hl[:, n % 4, :], ha[:, n % 2, :], hh[:, n % 4, :].bitcast(F32),
                                                ALU.subtract).then_inc(hl_ready, 1)
                accumulate(E * GROUPS - 1)
                for b in range(NB):
                    tiles = x1[:, b * TPB:(b + 1) * TPB, :]
                    dve.wait_ge(acc_tr, b + 1)
                    nc.vector.tensor_tensor(tiles, tiles, (tr_ps, ro_ps)[b % 2][:, :].rearrange(
                        "p (t d) -> p t d", d=P), ALU.add).then_inc(out_ready, 1)

            @block2.scalar
            def _(act):
                for b in range(NB):
                    cols = slice(b * S, (b + 1) * S)
                    act.wait_ge(x3_tr, b + 1)
                    nc.scalar.activation(x3T[:, cols], ro_ps[:, :], ACT.Copy).then_inc(x3T_ready, 1)
                    nc.scalar.activation(x3h[:, cols], ro_ps[:, :], ACT.Copy).then_inc(x3h_ready, 1)
                    act.wait_ge(logit_max, b + 1)
                    nc.scalar.activation(pr[:, :, :], pr[:, :, :], ACT.Exp).then_inc(prob_exp, 1)
                    act.wait_ge(comb_tr, b + 1)
                    if b >= 2:
                        act.wait_ge(rows_out[b - 2], 16)
                    nc.scalar.activation(combT[:, b % 2, :], ro_ps[0:E, :], ACT.Copy).then_inc(combT_ready, 1)
                for n in range(E * GROUPS * FC):
                    act.wait_ge(gate_mm, n + 1)
                    if n >= 2:
                        act.wait_ge(ha_ready, n - 1)
                    nc.scalar.activation(gl[:, n % 2, :], gate_ps[:, n % 2, :], ACT.Gelu).then_inc(gelu_done, 1)
                    act.wait_ge(ha_ready, n + 1)
                    if n >= 4:
                        act.wait_ge(down_mm, (n - 4) // FC + 1 if (n - 4) % FC == FC - 1 else (n - 4) // FC)
                    nc.scalar.activation(hh[:, n % 4, :], ha[:, n % 2, :], ACT.Copy).then_inc(hh_ready, 1)

            @block2.tensor
            def _(pe):
                def product(dst, wh, wl, mh, ml, start, stop):
                    nc.tensor.matmul(dst, wh, mh, start=start, stop=False)
                    nc.tensor.matmul(dst, wl, mh, start=False, stop=False)
                    return nc.tensor.matmul(dst, wh, ml, start=False, stop=stop)

                for b in range(NB):
                    if b >= 1:
                        pe.wait_ge(ln_stats, LN_DONE + 2 * b)
                    for t in range(TPB):
                        last = nc.tensor.transpose(tr_ps[:, t * P:(t + 1) * P],
                                                   yT[:, b * S + t * P:b * S + (t + 1) * P], ident[:, :])
                    last.then_inc(yT_tr, 1)
                    pe.wait_ge(x3_ready, b + 1)
                    if b >= 1:
                        pe.wait_ge(combT_ready, b)
                    for t in range(TPB):
                        last = nc.tensor.transpose(ro_ps[:, t * P:(t + 1) * P], x3[:, t, :], ident[:, :])
                    last.then_inc(x3_tr, 1)
                    pe.wait_ge(x3h_ready, b + 1)
                    if b == 0:
                        pe.wait_ge(consts2_in, 64)
                    for t in range(TPB):
                        last = nc.tensor.matmul(ro_ps[:, t * E:(t + 1) * E],
                                                x3T[:, b * S + t * P:b * S + (t + 1) * P], gw[:, :],
                                                start=True, stop=True)
                    last.then_inc(logit_mm, 1)
                    pe.wait_ge(comb_ready, b + 1)
                    for t in range(TPB):
                        last = nc.tensor.transpose(ro_ps[0:E, t * P:(t + 1) * P], comb[:, t, :], ident[:, :])
                    last.then_inc(comb_tr, 1)
                pe.wait_ge(x3l_ready, NB)

                def down(n):
                    k, fc = divmod(n, FC)
                    e = k // GROUPS
                    pe.wait_ge(hl_ready, n + 1)
                    if fc == 0 and k >= 2:
                        pe.wait_ge(acc_done, k - 1)
                    last = product(down_ps[:, k % 2, :], wdnh[:, e % 2, fc, :], wdnl[:, e % 2, fc, :],
                                   hh[:, n % 4, :], hl[:, n % 4, :], fc == 0, fc == FC - 1)
                    if fc == FC - 1:
                        last.then_inc(down_mm, 1)

                LAG = 2
                for n in range(E * GROUPS * FC):
                    k, fc = divmod(n, FC)
                    e, g = divmod(k, GROUPS)
                    cols = slice(g * S, (g + 1) * S)
                    if g == 0 and fc == 0:
                        pe.wait_ge(w_split, 2 * (e + 1))
                    if n >= 2:
                        pe.wait_ge(gelu_done, n - 1)
                    fcols = slice(fc * P, (fc + 1) * P)
                    product(gate_ps[:, n % 2, :], wguh[:, e % 2, fcols], wgul[:, e % 2, fcols], x3h[:, cols],
                            x3l[:, cols], True, True).then_inc(gate_mm, 1)
                    if fc == 0:
                        pe.wait_ge(xel_ready, k + 1)
                    if n >= 2:
                        pe.wait_ge(ha_ready, n - 1)
                    ucols = slice(F + fc * P, F + (fc + 1) * P)
                    product(up_ps[:, n % 2, :], wguh[:, e % 2, ucols], wgul[:, e % 2, ucols], xeh[:, k % 2, :],
                            xel[:, k % 2, :], True, True).then_inc(up_mm, 1)
                    if n >= LAG:
                        down(n - LAG)
                for n in range(E * GROUPS * FC - LAG, E * GROUPS * FC):
                    down(n)
                for b in range(NB):
                    pe.wait_ge(acc_done, (E - 1) * GROUPS + b + 1)
                    if b >= 2:
                        pe.wait_ge(out_ready, b - 1)
                    for t in range(TPB):
                        last = nc.tensor.transpose((tr_ps, ro_ps)[b % 2][:, t * P:(t + 1) * P],
                                                   acc[:, b * S + t * P:b * S + (t + 1) * P], ident[:, :])
                    last.then_inc(acc_tr, 1)


def constants():
    import numpy as np

    eye = np.eye(P, dtype=np.float32)
    head_rows = np.zeros((P, UP, P), np.float32)
    for i in range(UH):
        head_rows[32 * (i % 4) + i // 4, i // 2, DH * (i % 2):DH * (i % 2) + DH] = 1.0
    sum_rows = np.ones((P, 2, 32), np.float32)
    sum_rows[:, 0, 1] = 0.0
    sum_rows[:, 1, 0] = 0.0
    lower = np.ascontiguousarray(np.broadcast_to(np.tril(np.ones((8, 8), np.float32), -1), (P, 8, 8)))
    return {"eye": eye, "head_rows": head_rows, "sum_rows": sum_rows, "lower": lower}


def kernel(**inputs):
    import numpy as _np
    import concourse.bacc as _bacc
    from concourse import mybir as _mybir
    from concourse.bass_utils import run_bass_kernel_spmd as _run

    def plain(name):
        return _np.ascontiguousarray(inputs[name])

    def turned(name, *axes):
        return _np.ascontiguousarray(_np.transpose(_np.asarray(inputs[name]), axes))

    data = {
        "x": plain("L0_attn_x"), "ln1_g": plain("L0_attn_ln1_g"), "ln1_b": plain("L0_attn_ln1_b"),
        "wq": plain("L0_attn_Wq"), "wkv": plain("L0_attn_Wkv"), "wo": plain("L0_attn_Wo"),
        "ln2_g": plain("L0_attn_ln2_g"), "ln2_b": plain("L0_attn_ln2_b"),
        "gate_wT": turned("L0_ffn_gate_w", 1, 0), "gate_upT": turned("L0_ffn_gate_up_w", 0, 2, 1),
        "downT": turned("L0_ffn_down_w", 0, 2, 1), **constants(),
    }
    nc = _bacc.Bacc("TRN2", target_bir_lowering=False, num_devices=1)
    arrays, args = {}, []
    for name, a in data.items():
        arrays[f"in_{name}"] = a
        args.append(nc.dram_tensor(f"in_{name}", a.shape, _mybir.dt.from_np(a.dtype), kind="ExternalInput").ap())
    out = nc.dram_tensor("out_0", data["x"].shape, F32, kind="ExternalOutput").ap()
    bass_preln_mqa_moe_kernel(nc, *args, out)
    r = _run(nc, [arrays], core_ids=[0])
    return r.results[0]["out_0"]
```

```python
from contextlib import ExitStack

import concourse.bass as bass
from concourse import mybir

F32 = mybir.dt.float32
F32R = mybir.dt.float32r
ALU = mybir.AluOpType
ACT = mybir.ActivationFunctionType
AX_X = mybir.AxisListType.X

P = 128
HEADS = 16
DH = 64
EPS = 1e-5
UH = 8
UP = UH // 2
JT = 4
TOP_K = 2
SUM_SLOTS = 6
RAW_SLOTS = 5


def attention_schedule(units):
    prepare = ("STAT0", "APPLY0", "STAT1", "APPLY1", "XT", "XL", "K", "KL", "V", "VC")
    prepare_at = dict(zip(prepare, (0, 2, 4, 6, 9, 10, 11, 12, 16, 17)))
    after_at = dict(zip(AFTER_STEPS, (3, 4, 6, 8, 10, 15, 17, 18, 20, 23)))
    steps = [(kind, 0, 0) for kind in prepare]
    for p in range(UP):
        steps += [("Q", 0, p), ("QLO", 0, p)] + [("MAX", 0, 4 * p + s) for s in range(4)]
    steps.append(("SHIFT", 0, 0))
    if units > 1:
        steps += [("Q", 1, 0), ("QLO", 1, 0)]
    slots = UH * JT
    for u in range(units + 1):
        for n in range(slots):
            i, jt = divmod(n, JT)
            if u < units:
                steps.append(("EXP", u, n))
            if u + 1 < units:
                for s in range(2 * UH):
                    if (3 * s) // 2 == n:
                        steps.append(("MAX", u + 1, s))
                if n in (1, 7, 13):
                    steps.append(("Q", u + 1, n // 6 + 1))
                if n in (2, 8, 14):
                    steps.append(("QLO", u + 1, n // 6 + 1))
                if n == 26:
                    steps.append(("SHIFT", u + 1, 0))
            if u + 2 < units and n == 29:
                steps.append(("Q", u + 2, 0))
            if u + 2 < units and n == 30:
                steps.append(("QLO", u + 2, 0))
            if u % 2 == 0 and u + 2 < units:
                steps += [(kind, u // 2 + 1, 0) for kind in prepare if prepare_at[kind] == n]
            if u % 2 == 1 and 3 <= u < units:
                steps += [(kind, (u - 3) // 2, 0) for kind in AFTER_STEPS if after_at[kind] == n]
            if jt == 1:
                if i == 0 and u > 0:
                    steps.append(("PV", u - 1, UP - 1))
                elif i in (2, 4, 6) and u < units:
                    steps.append(("PV", u, i // 2 - 1))
            if jt == 2:
                if i == 0 and u > 0:
                    steps.append(("RAW", u - 1, UP - 1))
                elif i in (2, 4, 6) and u < units:
                    steps.append(("RAW", u, i // 2 - 1))
            if u > 0:
                if n == 7:
                    steps.append(("SUM", u - 1, 1))
                if n in (7, 8, 9, 10):
                    steps.append(("RECIP", u - 1, n - 7))
                if jt == 3 and 3 <= i <= 6:
                    steps.append(("NORM", u - 1, i - 3))
                if jt == 1 and 4 <= i <= 7:
                    steps.append(("LOW", u - 1, i - 4))
                if jt == 3 and 4 <= i <= 7:
                    steps.append(("OUT", u - 1, i - 4))
            if u < units and n == 30:
                steps.append(("SUM", u, 0))
    return steps


AFTER_STEPS = ("YT", "YSTAT", "YADD", "XSTAT", "XNORM", "X3T", "LOGIT", "CHOOSE0", "CHOOSE1", "ROWS")


def bass_preln_mqa_moe_kernel(nc, x, ln1_g, ln1_b, wq, wkv, wo, ln2_g, ln2_b, gate_wT, gate_upT, downT,
                              eye, head_rows, sum_rows, lower, out):
    NB, S, D = x.shape
    T = NB * S
    TPB = S // P
    E = gate_wT.shape[1]
    F = gate_upT.shape[2] // 2
    FC = F // P
    UNITS = NB * HEADS // UH
    PAIRS = HEADS // 2
    SCALE = float(DH) ** -0.5
    assert D == P and S == 4 * P and JT == TPB and UNITS == 2 * NB

    x_t = x.rearrange("b (t p) d -> b p t d", p=P)
    out_t = out.rearrange("b (t p) d -> b p t d", p=P)
    combine_rows = nc.dram_tensor("combine_rows", [E, T], F32).ap()
    steps = attention_schedule(UNITS)
    last_unit = UNITS - 1

    with ExitStack() as whole:
        def sb(stack, name, shape, dt=F32):
            return stack.enter_context(nc.sbuf_tensor(name, shape, dt))

        def ps(stack, name, shape):
            return stack.enter_context(nc.psum_tensor(name, shape, F32))

        def sem(name):
            return whole.enter_context(nc.semaphore(name))

        ident = sb(whole, "ident", [P, P])
        minus_half = sb(whole, "minus_half", [P, TPB])
        stats = sb(whole, "stats", [P, TPB, 6])
        moments = sb(whole, "moments", [P, TPB, 2])
        var_eps = sb(whole, "var_eps", [P, TPB])
        rstd = sb(whole, "rstd", [P, TPB])
        x1 = sb(whole, "x1", [P, NB * TPB, P])
        yT = sb(whole, "yT", [P, S])
        z = sb(whole, "z", [P, TPB, P])
        x3 = sb(whole, "x3", [P, TPB, P])
        x3T = sb(whole, "x3T", [P, T])
        g2 = sb(whole, "g2", [P, P])
        b2 = sb(whole, "b2", [P, P])
        gw = sb(whole, "gw", [P, E])
        tri = sb(whole, "tri", [P, E, E])
        most = sb(whole, "most", [P, TPB])
        over = sb(whole, "over", [P, TPB])
        pr = sb(whole, "pr", [P, TPB, E])
        cmp = sb(whole, "cmp", [P, TPB, E, E])
        eqs = sb(whole, "eqs", [P, TPB, E, E])
        cnt = sb(whole, "cnt", [P, TPB, E])
        comb = sb(whole, "comb", [P, TPB, E])
        combT = sb(whole, "combT", [E, S])

        half_set = sem("half_set")
        x1_in = [sem(f"x1_in{b}") for b in range(NB)]
        consts_in = sem("consts_in")
        consts2_in = sem("consts2_in")
        ln_stats = sem("ln_stats")
        ln_rstd = sem("ln_rstd")
        dve_own = sem("dve_own")
        pool_own = sem("pool_own")
        y_ready = sem("y_ready")
        y_turned = sem("y_turned")
        z_ready = sem("z_ready")
        x3_ready = sem("x3_ready")
        x3_turned = sem("x3_turned")
        x3T_ready = sem("x3T_ready")
        logit_mm = sem("logit_mm")
        logit_less = sem("logit_less")
        prob_exp = sem("prob_exp")
        comb_ready = sem("comb_ready")
        comb_turned = sem("comb_turned")
        combT_ready = sem("combT_ready")
        rows_out = sem("rows_out")
        count = {"dve": 0, "pool": 0, "ln": 0, "ln_pool": 0}

        def link(dve, ins):
            ins.then_inc(dve_own, 1)
            count["dve"] += 1
            dve.wait_ge(dve_own, count["dve"])

        def link_pool(pool, ins):
            ins.then_inc(pool_own, 1)
            count["pool"] += 1
            pool.wait_ge(pool_own, count["pool"])

        def ln_moments(dve, tile):
            for t in range(TPB):
                last = nc.vector.bn_stats(stats[:, t, :], tile[:, t, :])
            link(dve, last)
            for t in range(TPB):
                last = nc.vector.bn_aggr(moments[:, t, :], stats[:, t, :])
            last.then_inc(ln_stats, 1)

        def ln_rsqrt(pool):
            count["ln_pool"] += 1
            pool.wait_ge(ln_stats, count["ln_pool"])
            link_pool(pool, nc.gpsimd.tensor_scalar(var_eps[:, :], moments[:, :, 1], 1.0, EPS, ALU.mult, ALU.add))
            nc.gpsimd.tensor_tensor(rstd[:, :], var_eps[:, :], minus_half[:, :], ALU.pow).then_inc(ln_rstd, 1)

        def ln_apply(dve, dst, src):
            count["ln"] += 1
            dve.wait_ge(ln_rstd, count["ln"])
            for t in range(TPB):
                last = nc.vector.tensor_scalar(dst[:, t, :], src[:, t, :], moments[:, t, 0:1], rstd[:, t:t + 1],
                                               ALU.subtract, ALU.mult)
            return last

        def after_bank_read(kind, b):
            return {"YT": (z_ready, b + 1), "X3T": (x3T_ready, b + 1), "LOGIT": (logit_less, b + 1),
                    "ROWS": (combT_ready, b + 1)}[kind]

        def after_tensor(pe, kind, b, bank):
            if kind == "YT":
                pe.wait_ge(y_ready, b + 1)
                for t in range(TPB):
                    last = nc.tensor.transpose(bank[:, t * P:(t + 1) * P], yT[:, t * P:(t + 1) * P], ident[:, :])
                last.then_inc(y_turned, 1)
            if kind == "X3T":
                pe.wait_ge(x3_ready, b + 1)
                for t in range(TPB):
                    last = nc.tensor.transpose(bank[:, t * P:(t + 1) * P], x3[:, t, :], ident[:, :])
                last.then_inc(x3_turned, 1)
            if kind == "LOGIT":
                pe.wait_ge(x3T_ready, b + 1)
                if b == 0:
                    pe.wait_ge(consts2_in, 64)
                for t in range(TPB):
                    last = nc.tensor.matmul(bank[:, t * E:(t + 1) * E], x3T[:, b * S + t * P:b * S + (t + 1) * P],
                                            gw[:, :], start=True, stop=True)
                last.then_inc(logit_mm, 1)
            if kind == "ROWS":
                pe.wait_ge(comb_ready, b + 1)
                for t in range(TPB):
                    last = nc.tensor.transpose(bank[0:E, t * P:(t + 1) * P], comb[:, t, :], ident[:, :])
                last.then_inc(comb_turned, 1)

        def after_scalar(act, kind, b, bank):
            if kind == "YT":
                act.wait_ge(y_turned, b + 1)
                nc.scalar.activation(z[:, :, :], bank[:, :].rearrange("p (t d) -> p t d", d=P),
                                     ACT.Copy).then_inc(z_ready, 1)
            if kind == "X3T":
                act.wait_ge(x3_turned, b + 1)
                nc.scalar.activation(x3T[:, b * S:(b + 1) * S], bank[:, :], ACT.Copy).then_inc(x3T_ready, 1)
            if kind == "CHOOSE0":
                act.wait_ge(logit_less, b + 1)
                nc.scalar.activation(pr[:, :, :], pr[:, :, :], ACT.Exp).then_inc(prob_exp, 1)
            if kind == "ROWS":
                act.wait_ge(comb_turned, b + 1)
                if b >= 1:
                    act.wait_ge(rows_out, 16 * b)
                nc.scalar.activation(combT[:, :], bank[0:E, :], ACT.Copy).then_inc(combT_ready, 1)

        def after_gpsimd(pool, kind):
            if kind in ("YSTAT", "XSTAT"):
                ln_rsqrt(pool)

        def after_vector(dve, kind, b, bank):
            tiles = x1[:, b * TPB:(b + 1) * TPB, :]
            if kind == "YSTAT":
                dve.wait_ge(z_ready, b + 1)
                ln_moments(dve, z)
            if kind == "YADD":
                link(dve, ln_apply(dve, z, z))
                if b == 0:
                    dve.wait_ge(consts2_in, 64)
                link(dve, nc.vector.tensor_tensor(z[:, :, :], z[:, :, :],
                                                  g2[:, :].unsqueeze(1).broadcast_to([P, TPB, P]), ALU.mult))
                link(dve, nc.vector.tensor_tensor(z[:, :, :], z[:, :, :],
                                                  b2[:, :].unsqueeze(1).broadcast_to([P, TPB, P]), ALU.add))
                link(dve, nc.vector.tensor_tensor(tiles, tiles, z[:, :, :], ALU.add))
            if kind == "XSTAT":
                ln_moments(dve, tiles)
            if kind == "XNORM":
                if b >= 1:
                    dve.wait_ge(x3_turned, b)
                ln_apply(dve, x3, tiles).then_inc(x3_ready, 1)
            if kind == "CHOOSE0":
                logits = bank[:, 0:TPB * E].rearrange("p (t e) -> p t e", e=E)
                dve.wait_ge(logit_mm, b + 1)
                link(dve, nc.vector.tensor_reduce(most[:, :], logits, AX_X, ALU.max))
                nc.vector.tensor_tensor(pr[:, :, :], logits, most[:, :].unsqueeze(2).broadcast_to([P, TPB, E]),
                                        ALU.subtract).then_inc(logit_less, 1)
            if kind == "CHOOSE1":
                dve.wait_ge(prob_exp, b + 1)
                link(dve, nc.vector.tensor_reduce(most[:, :], pr[:, :, :], AX_X, ALU.add))
                link(dve, nc.vector.reciprocal(over[:, :], most[:, :]))
                link(dve, nc.vector.tensor_tensor(pr[:, :, :], pr[:, :, :],
                                                  over[:, :].unsqueeze(2).broadcast_to([P, TPB, E]), ALU.mult))
                for t in range(TPB):
                    other = pr[:, t, :].unsqueeze(1).broadcast_to([P, E, E])
                    this = pr[:, t, :].unsqueeze(2).broadcast_to([P, E, E])
                    nc.vector.tensor_tensor(cmp[:, t], other, this, ALU.is_gt)
                    last = nc.vector.tensor_tensor(eqs[:, t], other, this, ALU.is_equal)
                link(dve, last)
                link(dve, nc.vector.tensor_tensor(eqs[:, :, :, :], eqs[:, :, :, :],
                                                  tri[:, :, :].unsqueeze(1).broadcast_to([P, TPB, E, E]), ALU.mult))
                link(dve, nc.vector.tensor_tensor(cmp[:, :, :, :], cmp[:, :, :, :], eqs[:, :, :, :], ALU.add))
                link(dve, nc.vector.tensor_reduce(cnt[:, :, :], cmp[:, :, :, :], AX_X, ALU.add))
                link(dve, nc.vector.tensor_scalar(cnt[:, :, :], cnt[:, :, :], TOP_K - 0.5, None, ALU.is_lt))
                link(dve, nc.vector.tensor_tensor(pr[:, :, :], pr[:, :, :], cnt[:, :, :], ALU.mult))
                link(dve, nc.vector.tensor_reduce(most[:, :], pr[:, :, :], AX_X, ALU.add))
                link(dve, nc.vector.reciprocal(over[:, :], most[:, :]))
                if b >= 1:
                    dve.wait_ge(comb_turned, b)
                nc.vector.tensor_tensor(comb[:, :, :], pr[:, :, :],
                                        over[:, :].unsqueeze(2).broadcast_to([P, TPB, E]),
                                        ALU.mult).then_inc(comb_ready, 1)

        def after_sync(sp, kind, b):
            if kind == "ROWS":
                sp.wait_ge(combT_ready, b + 1)
                sp.dma_start(combine_rows[:, b * S:(b + 1) * S], combT[:, :]).then_inc(rows_out, 16)

        with ExitStack() as att:
            gcol = sb(att, "gcol", [P, 1])
            bcol = sb(att, "bcol", [P, 1])
            xn = x3
            xnT = z[:, :, :].rearrange("p t d -> p (t d)")
            xh = sb(att, "xh", [P, 2, S], F32R)
            xl = sb(att, "xl", [P, 2, S], F32R)
            khh = sb(att, "khh", [P, 2, S], F32R)
            kly = sb(att, "kly", [P, 2, S], F32R)
            v = sb(att, "v", [P, 2, TPB, DH])
            wqh = sb(att, "wqh", [P, HEADS * DH], F32R)
            wql = sb(att, "wql", [P, HEADS * DH], F32R)
            wkh = sb(att, "wkh", [P, P], F32R)
            wkl = sb(att, "wkl", [P, P], F32R)
            wvh = sb(att, "wvh", [P, DH], F32R)
            wvl = sb(att, "wvl", [P, DH], F32R)
            woh = sb(att, "woh", [P, PAIRS, P], F32R)
            wol = sb(att, "wol", [P, PAIRS, P], F32R)
            q_hl = sb(att, "q_hl", [P, 2, UH, S], F32R)
            q_hm = sb(att, "q_hm", [P, 2, UH, S], F32R)
            rowmax = sb(att, "rowmax", [P, 2, TPB, UH])
            mrow = sb(att, "mrow", [UH, 2, S], F32R)
            prob = sb(att, "prob", [P, 4, JT, S])
            fold = sb(att, "fold", [P, 2, S])
            psums = sb(att, "psums", [P, SUM_SLOTS, S])
            sumsel = sb(att, "sumsel", [P, 2, 32])
            headsel = sb(att, "headsel", [P, UP, P], F32R)
            rih = sb(att, "rih", [P, S], F32R)
            ril = sb(att, "ril", [P, S], F32R)
            raw = sb(att, "raw", [P, RAW_SLOTS, S])
            ao = sb(att, "ao", [P, S])
            rinv = ao
            aoh = sb(att, "aoh", [P, 2, S], F32R)
            aol = sb(att, "aol", [P, 2, S], F32R)
            wq_raw = prob[:, 0, 0:2, :].rearrange("p a s -> p (a s)")
            wo_raw = prob[:, 0, 2:4, :].rearrange("p a (c n) -> p (a c) n", n=P)
            wk_raw = prob[:, 1, 0, 0:P]
            wv_raw = prob[:, 1, 0, P:P + DH]
            hs_raw = prob[:, 1, 1, :].rearrange("p (u n) -> p u n", n=P)

            q_ps = ps(att, "q_ps", [P, S])
            max_ps = ps(att, "max_ps", [P, 2, S])
            s_ps = ps(att, "s_ps", [P, 2, S])
            pv_ps = ps(att, "pv_ps", [P, S])
            sum_ps = ps(att, "sum_ps", [P, S])
            y_ps = ps(att, "y_ps", [P, S])

            names = """wkv_in wq_in wo_in ones_set wkv_split wq_split wo_split headsel_set
                xn_ready x_turned xnT_sb xh_ready xl_ready k_mm kh_ready kl_ready v_mm v_ready
                q_mm q_hi q_lo q_top max_mm max_done shift_mm mrow_ready score_mm exp_done
                pv_mm raw_ready prob_folded head_sum sum_mm recip_done norm_mm ao_ready aoh_ready ao_split
                out_mm""".split()
            (wkv_in, wq_in, wo_in, ones_set, wkv_split, wq_split, wo_split, headsel_set,
             xn_ready, x_turned, xnT_sb, xh_ready, xl_ready, k_mm, kh_ready, kl_ready, v_mm, v_ready,
             q_mm, q_hi, q_lo, q_top, max_mm, max_done, shift_mm, mrow_ready, score_mm, exp_done,
             pv_mm, raw_ready, prob_folded, head_sum, sum_mm, recip_done, norm_mm, ao_ready, aoh_ready, ao_split,
             out_mm) = [sem(n) for n in names]
            mrow_in = [sem(f"mrow_in{n}") for n in range(2)]

            def vector_sums(head):
                return head // UH == last_unit and head % 2 == 1

            gpsimd_heads = [h for h in range(UNITS * UH) if not vector_sums(h)]
            vector_heads = [h for h in range(UNITS * UH) if vector_sums(h)]
            vec_sum = sem("vec_sum")

            def sums_done(eng, heads):
                eng.wait_ge(head_sum, sum(h < heads for h in gpsimd_heads))
                if any(h < heads for h in vector_heads):
                    eng.wait_ge(vec_sum, sum(h < heads for h in vector_heads))

            block = att.enter_context(nc.Block())

            @block.sync
            def _(sp):
                sp.dma_start(x1[:, 0:TPB, :], x_t[0]).then_inc(x1_in[0], 16)
                for dst, src in ((ident[:, :], eye), (gcol[:, :], ln1_g.rearrange("(p o) -> p o", o=1)),
                                 (bcol[:, :], ln1_b.rearrange("(p o) -> p o", o=1)),
                                 (hs_raw, head_rows), (sumsel[:, :, :], sum_rows)):
                    sp.dma_start(dst, src).then_inc(consts_in, 16)
                sp.dma_start(wk_raw[:, 0:DH], wkv[:, 0:DH]).then_inc(wkv_in, 16)
                sp.dma_start(wk_raw[:, DH:P], wkv[:, 0:DH]).then_inc(wkv_in, 16)
                sp.dma_start(wv_raw, wkv[:, DH:2 * DH]).then_inc(wkv_in, 16)
                sp.dma_start(wq_raw, wq).then_inc(wq_in, 16)
                sp.dma_start(wo_raw, wo.rearrange("(c p) n -> p c n", p=P)).then_inc(wo_in, 16)
                for b in range(1, NB):
                    sp.dma_start(x1[:, b * TPB:(b + 1) * TPB, :], x_t[b]).then_inc(x1_in[b], 16)
                for dst, src in ((g2[:, :], ln2_g.partition_broadcast(P)), (b2[:, :], ln2_b.partition_broadcast(P)),
                                 (gw[:, :], gate_wT), (tri[:, :, :], lower)):
                    sp.dma_start(dst, src).then_inc(consts2_in, 16)
                for kind, u, _ in steps:
                    if kind == "SHIFT":
                        sp.wait_ge(mrow_ready, 2 * (u + 1))
                        if u >= 2:
                            sp.wait_ge(score_mm, (u - 1) * UH * JT)
                        for part in range(2):
                            sp.dma_start(q_hm[DH + part:DH + part + 1, u % 2, :, :].bitcast(F32),
                                         mrow[:, part, :].bitcast(F32)).then_inc(mrow_in[u % 2], 16)
                    if kind in AFTER_STEPS:
                        after_sync(sp, kind, u)
                sp.wait_ge(rows_out, 16 * (NB - 1))

            @block.gpsimd
            def _(pool):
                nc.gpsimd.memset(minus_half[:, :], -0.5).then_inc(half_set, 1)
                pool.wait_ge(half_set, 1)

                def split(raw_ap, high, low, done):
                    link_pool(pool, nc.gpsimd.tensor_scalar(high, raw_ap, 1.0, 1.0, ALU.mult, ALU.mult))
                    nc.gpsimd.tensor_tensor(low, raw_ap, high.bitcast(F32), ALU.subtract).then_inc(done, 1)

                for kind, u, a in steps:
                    if kind in ("STAT0", "STAT1"):
                        ln_rsqrt(pool)
                    if kind == "STAT1" and u == 0:
                        pool.wait_ge(wkv_in, 48)
                        split(wk_raw, wkh[:, :], wkl[:, :], wkv_split)
                        split(wv_raw, wvh[:, :], wvl[:, :], wkv_split)
                        pool.wait_ge(wq_in, 16)
                        for c in range(2):
                            half = slice(c * S, (c + 1) * S)
                            split(wq_raw[:, half], wqh[:, half], wql[:, half], wq_split)
                    if kind == "Q":
                        k = u * UP + a
                        pool.wait_ge(q_hi, 2 * (k + 1))
                        pair = slice(2 * a, 2 * a + 2)
                        nc.gpsimd.tensor_scalar(q_hm[0:DH, u % 2, pair, :], q_hl[0:DH, u % 2, pair, :].bitcast(F32),
                                                1.0, 1.0, ALU.mult, ALU.mult).then_inc(q_top, 1)
                        if k == 0:
                            pool.wait_ge(consts_in, 80)
                            nc.gpsimd.tensor_scalar(headsel[:, :, :], hs_raw, 1.0, 1.0, ALU.mult,
                                                    ALU.mult).then_inc(headsel_set, 1)
                            pool.wait_ge(wo_in, 16)
                            split(wo_raw, woh[:, :, :], wol[:, :, :], wo_split)
                    if kind == "EXP" and a % JT == JT - 1:
                        head = u * UH + a // JT
                        if not vector_sums(head):
                            done = gpsimd_heads.index(head)
                            pool.wait_ge(exp_done, (head + 1) * JT)
                            if done >= 1:
                                pool.wait_ge(head_sum, done)
                            nc.gpsimd.tensor_tensor(fold[:, :, :], prob[:, head % 4, 0:2, :],
                                                    prob[:, head % 4, 2:4, :], ALU.add).then_inc(prob_folded, 1)
                            pool.wait_ge(prob_folded, done + 1)
                            if head >= SUM_SLOTS:
                                pool.wait_ge(sum_mm, (head - SUM_SLOTS) // 4 + 1)
                            nc.gpsimd.tensor_tensor(psums[:, head % SUM_SLOTS, :], fold[:, 0, :], fold[:, 1, :],
                                                    ALU.add).then_inc(head_sum, 1)
                    if kind in AFTER_STEPS:
                        after_gpsimd(pool, kind)

            @block.vector
            def _(dve):
                nc.vector.memset(kly[DH:DH + 2, :, :].bitcast(F32), 1.0).then_inc(ones_set, 1)
                for kind, u, a in steps:
                    b = u
                    if kind == "STAT0":
                        dve.wait_ge(x1_in[b], 16)
                        ln_moments(dve, x1[:, b * TPB:(b + 1) * TPB, :])
                    if kind == "APPLY0":
                        if b >= 1:
                            dve.wait_ge(x_turned, b)
                        link(dve, ln_apply(dve, xn, x1[:, b * TPB:(b + 1) * TPB, :]))
                    if kind == "STAT1":
                        ln_moments(dve, xn)
                    if kind == "APPLY1":
                        ln_apply(dve, xn, xn).then_inc(xn_ready, 1)
                    if kind == "XT":
                        dve.wait_ge(x_turned, b + 1)
                        if b == 0:
                            dve.wait_ge(consts_in, 80)
                        else:
                            dve.wait_ge(xh_ready, b)
                            dve.wait_ge(xl_ready, b)
                        nc.vector.tensor_scalar(xnT[:, :], q_ps[:, :], gcol[:, :], bcol[:, :], ALU.mult,
                                                ALU.add).then_inc(xnT_sb, 1)
                    if kind == "XL":
                        dve.wait_ge(xh_ready, b + 1)
                        nc.vector.tensor_tensor(xl[:, b % 2, :], xnT[:, :], xh[:, b % 2, :].bitcast(F32),
                                                ALU.subtract).then_inc(xl_ready, 1)
                    if kind == "KL":
                        dve.wait_ge(kh_ready, b + 1)
                        nc.vector.tensor_tensor(kly[0:DH, b % 2, :], q_ps[0:DH, :], khh[0:DH, b % 2, :].bitcast(F32),
                                                ALU.subtract).then_inc(kl_ready, 1)
                    if kind == "VC":
                        dve.wait_ge(v_mm, b + 1)
                        nc.vector.tensor_copy(v[:, b % 2, :, :],
                                              q_ps[:, 0:TPB * DH].rearrange("p (t d) -> p t d", d=DH)
                                              ).then_inc(v_ready, 1)
                    if kind == "QLO":
                        for hd in range(2):
                            h = 2 * (u * UP + a) + hd
                            dve.wait_ge(q_hi, h + 1)
                            nc.vector.tensor_tensor(q_hl[DH:P, u % 2, 2 * a + hd, :], q_ps[DH * hd:DH * hd + DH, :],
                                                    q_hl[0:DH, u % 2, 2 * a + hd, :].bitcast(F32),
                                                    ALU.subtract).then_inc(q_lo, 1)
                    if kind == "MAX":
                        i, half = divmod(a, 2)
                        dve.wait_ge(max_mm, u * 2 * UH + a + 1)
                        if a == 0 and u >= 2:
                            dve.wait_ge(shift_mm, u - 1)
                        nc.vector.tensor_reduce(rowmax[:, u % 2, 2 * half:2 * half + 2, i], max_ps[:, :, :], AX_X,
                                                ALU.max).then_inc(max_done, 1)
                    if kind == "SHIFT":
                        dve.wait_ge(shift_mm, u + 1)
                        if u >= 1:
                            dve.wait_ge(mrow_in[(u - 1) % 2], 32 * ((u - 1) // 2 + 1))
                        nc.vector.tensor_scalar(mrow[:, 0, :], q_ps[0:UH, :], -1.0, None,
                                                ALU.mult).then_inc(mrow_ready, 1)
                        dve.wait_ge(mrow_ready, 2 * u + 1)
                        nc.vector.scalar_tensor_tensor(out=mrow[:, 1, :], in0=q_ps[0:UH, :], scalar=-1.0,
                                                       in1=mrow[:, 0, :].bitcast(F32), op0=ALU.mult,
                                                       op1=ALU.subtract).then_inc(mrow_ready, 1)
                    if kind == "EXP" and a % JT == JT - 1 and vector_sums(u * UH + a // JT):
                        head = u * UH + a // JT
                        dve.wait_ge(exp_done, (head + 1) * JT)
                        dve.wait_ge(sum_mm, (head - SUM_SLOTS) // 4 + 1)
                        nc.vector.tensor_reduce(psums[:, head % SUM_SLOTS, :],
                                                prob[:, head % 4, :, :].rearrange("p j s -> p s j"), AX_X,
                                                ALU.add).then_inc(vec_sum, 1)
                    if kind == "RECIP":
                        quarter = slice(a * P, (a + 1) * P)
                        if a == 0:
                            dve.wait_ge(sum_mm, 2 * (u + 1))
                            if u >= 1:
                                dve.wait_ge(aoh_ready, u * UP)
                                dve.wait_ge(ao_split, u * UP)
                        link(dve, nc.vector.reciprocal(rinv[:, quarter], sum_ps[:, quarter]))
                        if a == 3:
                            if u >= 1:
                                dve.wait_ge(norm_mm, u * UP)
                            link(dve, nc.vector.tensor_copy(rih[:, :], rinv[:, :]))
                            nc.vector.tensor_tensor(ril[:, :], rinv[:, :], rih[:, :].bitcast(F32),
                                                    ALU.subtract).then_inc(recip_done, 1)
                    if kind == "NORM":
                        k = u * UP + a
                        dve.wait_ge(norm_mm, k + 1)
                        dve.wait_ge(raw_ready, k + 1)
                        if a >= 1:
                            dve.wait_ge(ao_split, k)
                        else:
                            dve.wait_ge(recip_done, u + 1)
                        nc.vector.tensor_tensor(ao[:, :], sum_ps[:, :], raw[:, k % RAW_SLOTS, :],
                                                ALU.mult).then_inc(ao_ready, 1)
                    if kind == "LOW":
                        k = u * UP + a
                        dve.wait_ge(aoh_ready, k + 1)
                        nc.vector.tensor_tensor(aol[:, k % 2, :], ao[:, :], aoh[:, k % 2, :].bitcast(F32),
                                                ALU.subtract).then_inc(ao_split, 1)
                    if kind in AFTER_STEPS:
                        after_vector(dve, kind, b, q_ps)

            @block.scalar
            def _(act):
                for kind, u, a in steps:
                    b = u
                    if kind == "XT":
                        act.wait_ge(xnT_sb, b + 1)
                        if b >= 2:
                            act.wait_ge(q_mm, (b - 1) * PAIRS)
                        nc.scalar.activation(xh[:, b % 2, :], xnT[:, :], ACT.Copy).then_inc(xh_ready, 1)
                    if kind == "K":
                        act.wait_ge(k_mm, b + 1)
                        nc.scalar.activation(khh[:, b % 2, :], q_ps[:, :], ACT.Copy).then_inc(kh_ready, 1)
                    if kind == "Q":
                        act.wait_ge(q_mm, u * UP + a + 1)
                        if u >= 2:
                            act.wait_ge(score_mm, ((u - 2) * UH + 2 * a + 2) * JT)
                        for hd in range(2):
                            nc.scalar.activation(q_hl[0:DH, u % 2, 2 * a + hd, :], q_ps[DH * hd:DH * hd + DH, :],
                                                 ACT.Copy).then_inc(q_hi, 1)
                    if kind == "EXP":
                        k = u * UH * JT + a
                        head, jt = divmod(k, JT)
                        act.wait_ge(score_mm, k + 1)
                        if k == 0:
                            act.wait_ge(wkv_split, 2)
                            act.wait_ge(wq_split, 2)
                            act.wait_ge(headsel_set, 1)
                            act.wait_ge(wo_split, 1)
                        elif head >= 4 and jt == 0:
                            act.wait_ge(pv_mm, (head - 4) // 2 + 1)
                            if vector_sums(head - 4):
                                act.wait_ge(vec_sum, vector_heads.index(head - 4) + 1)
                            else:
                                act.wait_ge(prob_folded, gpsimd_heads.index(head - 4) + 1)
                        nc.scalar.activation(prob[:, head % 4, jt, :], s_ps[:, k % 2, :], ACT.Exp,
                                             scale=SCALE).then_inc(exp_done, 1)
                    if kind == "RAW":
                        k = u * UP + a
                        act.wait_ge(pv_mm, k + 1)
                        if k >= RAW_SLOTS:
                            act.wait_ge(ao_ready, k - RAW_SLOTS + 1)
                        nc.scalar.activation(raw[:, k % RAW_SLOTS, :], pv_ps[:, :], ACT.Copy).then_inc(raw_ready, 1)
                    if kind == "NORM":
                        k = u * UP + a
                        act.wait_ge(ao_ready, k + 1)
                        if k >= 2:
                            act.wait_ge(out_mm, k - 1)
                        nc.scalar.activation(aoh[:, k % 2, :], ao[:, :], ACT.Copy).then_inc(aoh_ready, 1)
                    if kind == "OUT" and (u * UP + a) % PAIRS == PAIRS - 1:
                        b = (u * UP + a) // PAIRS
                        act.wait_ge(out_mm, PAIRS * (b + 1))
                        if b >= 1:
                            act.wait_ge(y_turned, b)
                        nc.scalar.activation(yT[:, :], y_ps[:, :], ACT.Copy).then_inc(y_ready, 1)
                    if kind in AFTER_STEPS:
                        after_scalar(act, kind, b, q_ps)

            @block.tensor
            def _(pe):
                def product(dst, wh, wl, mh, ml, start, stop):
                    nc.tensor.matmul(dst, wh, mh, start=start, stop=False, skip_group_check=True)
                    nc.tensor.matmul(dst, wl, mh, start=False, stop=False, skip_group_check=True)
                    return nc.tensor.matmul(dst, wh, ml, start=False, stop=stop, skip_group_check=True)

                def bank_read(kind, u, a):
                    if kind in AFTER_STEPS:
                        return after_bank_read(kind, u)
                    return {"XT": (xnT_sb, u + 1), "K": (kl_ready, u + 1), "V": (v_ready, u + 1),
                            "Q": (q_lo, 2 * (u * UP + a + 1)), "SHIFT": (mrow_ready, 2 * (u + 1))}[kind]

                pe.wait_ge(consts_in, 80)
                in_bank = None
                for kind, u, a in steps:
                    b = u // 2
                    if kind in ("XT", "K", "V", "Q", "SHIFT", "YT", "X3T", "LOGIT", "ROWS"):
                        if in_bank:
                            pe.wait_ge(*bank_read(*in_bank))
                        in_bank = (kind, u, a)
                    if kind == "XT":
                        pe.wait_ge(xn_ready, u + 1)
                        for t in range(TPB):
                            last = nc.tensor.transpose(q_ps[:, t * P:(t + 1) * P], xn[:, t, :], ident[:, :])
                        last.then_inc(x_turned, 1)
                    if kind == "K":
                        pe.wait_ge(xl_ready, u + 1)
                        if u == 0:
                            pe.wait_ge(wkv_split, 2)
                        product(q_ps[:, :], wkh[:, :], wkl[:, :], xh[:, u % 2, :], xl[:, u % 2, :],
                                True, True).then_inc(k_mm, 1)
                    if kind == "V":
                        for t in range(TPB):
                            tile = slice(t * P, (t + 1) * P)
                            last = product(q_ps[:, t * DH:(t + 1) * DH], xh[:, u % 2, tile], xl[:, u % 2, tile],
                                           wvh[:, :], wvl[:, :], t == 0, t == TPB - 1)
                        last.then_inc(v_mm, 1)
                    if kind == "Q":
                        c = (u * UP + a) % PAIRS
                        if u == 0 and a == 0:
                            pe.wait_ge(wq_split, 2)
                        wcols = slice(c * P, (c + 1) * P)
                        product(q_ps[:, :], wqh[:, wcols], wql[:, wcols], xh[:, b % 2, :], xl[:, b % 2, :],
                                True, True).then_inc(q_mm, 1)
                    if kind == "MAX":
                        i, half = divmod(a, 2)
                        k = u * 2 * UH + a
                        pe.wait_ge(q_lo, u * UH + i + 1)
                        if k >= 1:
                            pe.wait_ge(max_done, k)
                        for w in range(2):
                            it = 2 * half + w
                            last = nc.tensor.matmul(max_ps[:, w, :], q_hl[:, u % 2, i, it * P:(it + 1) * P],
                                                    khh[:, b % 2, :], start=True, stop=True)
                        last.then_inc(max_mm, 1)
                    if kind == "SHIFT":
                        pe.wait_ge(max_done, (u + 1) * 2 * UH)
                        for t in range(TPB):
                            last = nc.tensor.transpose(q_ps[0:UH, t * P:(t + 1) * P], rowmax[:, u % 2, t, :],
                                                       ident[:, :])
                        last.then_inc(shift_mm, 1)
                    if kind == "EXP":
                        k = u * UH * JT + a
                        i, jt = divmod(a, JT)
                        if k == 0:
                            pe.wait_ge(ones_set, 1)
                        if a == 0 and u % 2 == 0:
                            pe.wait_ge(kl_ready, b + 1)
                        if a == 0:
                            pe.wait_ge(mrow_in[u % 2], 32 * (u // 2 + 1))
                        if a % (2 * JT) == 0:
                            pe.wait_ge(q_top, u * UP + i // 2 + 1)
                        if k >= 2:
                            pe.wait_ge(exp_done, k - 1)
                        keys = slice(jt * P, (jt + 1) * P)
                        nc.tensor.matmul(s_ps[:, k % 2, :], khh[:, b % 2, keys], q_hl[:, u % 2, i, :],
                                         start=True, stop=False)
                        nc.tensor.matmul(s_ps[:, k % 2, :], kly[0:DH + 2, b % 2, keys],
                                         q_hm[0:DH + 2, u % 2, i, :],
                                         start=False, stop=True).then_inc(score_mm, 1)
                    if kind == "PV":
                        k = u * UP + a
                        pe.wait_ge(exp_done, (k + 1) * 2 * JT)
                        if a == 0:
                            pe.wait_ge(v_ready, b + 1)
                        if k >= 1:
                            pe.wait_ge(raw_ready, k)
                        for jt in range(JT):
                            for hd in range(2):
                                head = 2 * k + hd
                                last = nc.tensor.matmul(pv_ps[DH * hd:DH * hd + DH, :], v[:, b % 2, jt, :],
                                                        prob[:, head % 4, jt, :], start=(jt == 0),
                                                        stop=(jt == JT - 1))
                        last.then_inc(pv_mm, 1)
                    if kind == "SUM":
                        k = 2 * u + a
                        sums_done(pe, 4 * (k + 1))
                        if a == 0 and u >= 1:
                            pe.wait_ge(ao_ready, u * UP)
                        for i in range(4):
                            last = nc.tensor.matmul(sum_ps[32 * i:32 * i + 32, :], sumsel[:, a, :],
                                                    psums[:, (4 * k + i) % SUM_SLOTS, :], start=(a == 0),
                                                    stop=(a == 1), skip_group_check=True)
                        last.then_inc(sum_mm, 1)
                    if kind == "NORM":
                        k = u * UP + a
                        pe.wait_ge(recip_done, u + 1)
                        if k >= 1:
                            pe.wait_ge(ao_ready, k)
                        nc.tensor.matmul(sum_ps[:, :], headsel[:, a, :], rih[:, :], start=True, stop=False)
                        nc.tensor.matmul(sum_ps[:, :], headsel[:, a, :], ril[:, :], start=False,
                                         stop=True).then_inc(norm_mm, 1)
                    if kind == "OUT":
                        k = u * UP + a
                        c = k % PAIRS
                        pe.wait_ge(ao_split, k + 1)
                        if c == 0 and b >= 1:
                            pe.wait_ge(y_ready, b)
                        product(y_ps[:, :], woh[:, c, :], wol[:, c, :], aoh[:, k % 2, :], aol[:, k % 2, :],
                                c == 0, c == PAIRS - 1).then_inc(out_mm, 1)
                    if kind in AFTER_STEPS:
                        after_tensor(pe, kind, u, q_ps)

        with ExitStack() as moe:
            x3h = sb(moe, "x3h", [P, T], F32R)
            x3l = sb(moe, "x3l", [P, T], F32R)
            wgu_raw = sb(moe, "wgu_raw", [P, 2, 2 * F])
            wdn_raw = sb(moe, "wdn_raw", [P, 2, FC, P])
            wguh = sb(moe, "wguh", [P, 2, 2 * F], F32R)
            wgul = sb(moe, "wgul", [P, 2, 2 * F], F32R)
            wdnh = sb(moe, "wdnh", [P, 2, FC, P], F32R)
            wdnl = sb(moe, "wdnl", [P, 2, FC, P], F32R)
            cb = sb(moe, "cb", [P, 4, S])
            xe = sb(moe, "xe", [P, 2, S])
            xeh = sb(moe, "xeh", [P, 2, S], F32R)
            xel = sb(moe, "xel", [P, 2, S], F32R)
            gl = sb(moe, "gl", [P, 2, S])
            ha = sb(moe, "ha", [P, 3, S])
            hh = sb(moe, "hh", [P, 4, S], F32R)
            hl = sb(moe, "hl", [P, 4, S], F32R)
            acc = sb(moe, "acc", [P, T])

            gate_ps = ps(moe, "gate_ps", [P, 2, S])
            up_ps = ps(moe, "up_ps", [P, 2, S])
            down_ps = ps(moe, "down_ps", [P, 2, S])
            turn_ps = [ps(moe, f"turn_ps{n}", [P, S]) for n in range(2)]
            bank = turn_ps[0]

            names = """w_split x3h_ready x3l_ready xe_ready xeh_ready xel_ready gate_mm up_mm gelu_done ha_ready
                hh_ready hl_ready down_mm acc_done acc_turned out_ready out_sent""".split()
            (w_split, x3h_ready, x3l_ready, xe_ready, xeh_ready, xel_ready, gate_mm, up_mm, gelu_done, ha_ready,
             hh_ready, hl_ready, down_mm, acc_done, acc_turned, out_ready, out_sent) = [sem(n) for n in names]
            gu_in = [sem(f"gu_in{n}") for n in range(2)]
            dn_in = [sem(f"dn_in{n}") for n in range(2)]
            cb_in = [sem(f"cb_in{n}") for n in range(4)]
            GROUPS = NB
            KS = E * GROUPS
            NS = KS * FC
            LB = NB - 1
            AFTER_AT = dict(zip(AFTER_STEPS, (0, 0, 1, 2, 3, 5, 6, 6, 8, 10)))
            SPLIT_AT = {0: 0, 2: 1, 6: 2, 7: 3}
            DOWN_LAG = 3

            def after_steps(n):
                return [kind for kind in AFTER_STEPS if AFTER_AT[kind] == n]

            def down_done(eng, n):
                eng.wait_ge(down_mm, n + 1)

            block2 = moe.enter_context(nc.Block())

            @block2.sync
            def _(sp):
                def weights(e):
                    if e >= 2:
                        sp.wait_ge(w_split, 2 * (e - 1))
                    sp.dma_start(wgu_raw[:, e % 2, :], gate_upT[e]).then_inc(gu_in[e % 2], 16)
                    sp.dma_start(wdn_raw[:, e % 2, :, :],
                                 downT[e].rearrange("(c p) n -> p c n", p=P)).then_inc(dn_in[e % 2], 16)

                def combine(k):
                    e, g = divmod(k, GROUPS)
                    if k >= 4:
                        sp.wait_ge(xe_ready, k - 3)
                    sp.dma_start(cb[:, k % 4, :],
                                 combine_rows[e, g * S:(g + 1) * S].partition_broadcast(P)).then_inc(cb_in[k % 4], 16)

                weights(0)
                for k in range(LB):
                    combine(k)
                weights(1)
                after_sync(sp, "ROWS", LB)
                sp.wait_ge(rows_out, 16 * NB)
                for k in range(LB, KS):
                    combine(k)
                    if k % GROUPS == 0 and k // GROUPS + 1 < E:
                        weights(k // GROUPS + 1)
                for b in range(NB):
                    sp.wait_ge(out_ready, b + 1)
                    sp.dma_start(out_t[b], x1[:, b * TPB:(b + 1) * TPB, :]).then_inc(out_sent, 16)
                sp.wait_ge(out_sent, 16 * NB)

            @block2.gpsimd
            def _(pool):
                def split_weights(e):
                    for raw_in, raw_ap, high, low in (
                            (gu_in, wgu_raw[:, e % 2, :], wguh[:, e % 2, :], wgul[:, e % 2, :]),
                            (dn_in, wdn_raw[:, e % 2, :, :], wdnh[:, e % 2, :, :], wdnl[:, e % 2, :, :])):
                        pool.wait_ge(raw_in[e % 2], 16 * (e // 2 + 1))
                        if e >= 2:
                            pool.wait_ge(down_mm, (e - 1) * GROUPS * FC)
                        link_pool(pool, nc.gpsimd.tensor_scalar(high, raw_ap, 1.0, 1.0, ALU.mult, ALU.mult))
                        nc.gpsimd.tensor_tensor(low, raw_ap, high.bitcast(F32), ALU.subtract).then_inc(w_split, 1)

                def split_scaled(k):
                    pool.wait_ge(xe_ready, k + 1)
                    if k >= 2:
                        pool.wait_ge(up_mm, (k - 1) * FC)
                    nc.gpsimd.tensor_scalar(xeh[:, k % 2, :], xe[:, k % 2, :], 1.0, 1.0, ALU.mult,
                                            ALU.mult).then_inc(xeh_ready, 1)
                    pool.wait_ge(xeh_ready, k + 1)
                    nc.gpsimd.tensor_tensor(xel[:, k % 2, :], xe[:, k % 2, :], xeh[:, k % 2, :].bitcast(F32),
                                            ALU.subtract).then_inc(xel_ready, 1)

                split_weights(0)
                split_scaled(0)
                for n in range(NS):
                    k, fc = divmod(n, FC)
                    for kind in after_steps(n):
                        after_gpsimd(pool, kind)
                    if fc == 1 and k + 1 < KS:
                        split_scaled(k + 1)
                    if k % GROUPS == 1 and fc == 2 and k // GROUPS + 1 < E:
                        split_weights(k // GROUPS + 1)

            @block2.vector
            def _(dve):
                def scale_x(k):
                    g = k % GROUPS
                    dve.wait_ge(cb_in[k % 4], 16 * (k // 4 + 1))
                    if g == LB:
                        dve.wait_ge(x3T_ready, NB)
                    if k >= 2:
                        dve.wait_ge(xel_ready, k - 1)
                    nc.vector.tensor_tensor(xe[:, k % 2, :], x3T[:, g * S:(g + 1) * S], cb[:, k % 4, :],
                                            ALU.mult).then_inc(xe_ready, 1)

                def accumulate(k):
                    e, g = divmod(k, GROUPS)
                    cols = slice(g * S, (g + 1) * S)
                    dve.wait_ge(down_mm, (k + 1) * FC)
                    if e == 0:
                        nc.vector.tensor_copy(acc[:, cols], down_ps[:, k % 2, :]).then_inc(acc_done, 1)
                    else:
                        dve.wait_ge(acc_done, k - GROUPS + 1)
                        nc.vector.tensor_tensor(acc[:, cols], acc[:, cols], down_ps[:, k % 2, :],
                                                ALU.add).then_inc(acc_done, 1)

                def low_part(n):
                    dve.wait_ge(hh_ready, n + 1)
                    nc.vector.tensor_tensor(hl[:, n % 4, :], ha[:, n % 3, :], hh[:, n % 4, :].bitcast(F32),
                                            ALU.subtract).then_inc(hl_ready, 1)

                scale_x(0)
                for n in range(NS):
                    k, fc = divmod(n, FC)
                    for kind in after_steps(n):
                        after_vector(dve, kind, LB, bank)
                    if n in SPLIT_AT:
                        g = SPLIT_AT[n]
                        dve.wait_ge(x3h_ready, g + 1)
                        nc.vector.tensor_tensor(x3l[:, g * S:(g + 1) * S], x3T[:, g * S:(g + 1) * S],
                                                x3h[:, g * S:(g + 1) * S].bitcast(F32),
                                                ALU.subtract).then_inc(x3l_ready, 1)
                    dve.wait_ge(gelu_done, n + 1)
                    dve.wait_ge(up_mm, n + 1)
                    if n >= 3:
                        dve.wait_ge(hl_ready, n - 2)
                    nc.vector.tensor_tensor(ha[:, n % 3, :], up_ps[:, n % 2, :], gl[:, n % 2, :],
                                            ALU.mult).then_inc(ha_ready, 1)
                    if n >= 1:
                        low_part(n - 1)
                    if fc == (2 if k == LB - 1 else 0) and k + 1 < KS:
                        scale_x(k + 1)
                    if fc == 3 and k >= 1:
                        accumulate(k - 1)
                low_part(NS - 1)
                accumulate(KS - 1)
                for b in range(NB):
                    tiles = x1[:, b * TPB:(b + 1) * TPB, :]
                    dve.wait_ge(acc_turned, b + 1)
                    nc.vector.tensor_tensor(tiles, tiles, turn_ps[b % 2][:, :].rearrange("p (t d) -> p t d", d=P),
                                            ALU.add).then_inc(out_ready, 1)

            @block2.scalar
            def _(act):
                def high_part(n):
                    act.wait_ge(ha_ready, n + 1)
                    if n >= 4:
                        down_done(act, n - 4)
                    nc.scalar.activation(hh[:, n % 4, :], ha[:, n % 3, :], ACT.Copy).then_inc(hh_ready, 1)

                for n in range(NS):
                    for kind in after_steps(n):
                        after_scalar(act, kind, LB, bank)
                    if n in SPLIT_AT:
                        g = SPLIT_AT[n]
                        nc.scalar.activation(x3h[:, g * S:(g + 1) * S], x3T[:, g * S:(g + 1) * S],
                                             ACT.Copy).then_inc(x3h_ready, 1)
                    act.wait_ge(gate_mm, n + 1)
                    if n >= 2:
                        act.wait_ge(ha_ready, n - 1)
                    nc.scalar.activation(gl[:, n % 2, :], gate_ps[:, n % 2, :], ACT.Gelu).then_inc(gelu_done, 1)
                    if n >= 1:
                        high_part(n - 1)
                high_part(NS - 1)

            @block2.tensor
            def _(pe):
                def product(dst, wh, wl, mh, ml, start, stop):
                    nc.tensor.matmul(dst, wh, mh, start=start, stop=False)
                    nc.tensor.matmul(dst, wl, mh, start=False, stop=False)
                    return nc.tensor.matmul(dst, wh, ml, start=False, stop=stop)

                def down(n):
                    k, fc = divmod(n, FC)
                    e = k // GROUPS
                    pe.wait_ge(hl_ready, n + 1)
                    if fc == 0 and k >= 2:
                        pe.wait_ge(acc_done, k - 1)
                    product(down_ps[:, k % 2, :], wdnh[:, e % 2, fc, :], wdnl[:, e % 2, fc, :],
                            hh[:, n % 4, :], hl[:, n % 4, :], fc == 0, fc == FC - 1).then_inc(down_mm, 1)

                in_bank = None
                for n in range(NS):
                    k, fc = divmod(n, FC)
                    e, g = divmod(k, GROUPS)
                    cols = slice(g * S, (g + 1) * S)
                    for kind in after_steps(n):
                        if kind in ("YT", "X3T", "LOGIT", "ROWS"):
                            if in_bank:
                                pe.wait_ge(*after_bank_read(in_bank, LB))
                            in_bank = kind
                        after_tensor(pe, kind, LB, bank)
                    if g == 0 and fc == 0:
                        pe.wait_ge(w_split, 2 * (e + 1))
                    if e == 0 and fc == 0:
                        pe.wait_ge(x3l_ready, g + 1)
                    if n >= 2:
                        pe.wait_ge(gelu_done, n - 1)
                    fcols = slice(fc * P, (fc + 1) * P)
                    product(gate_ps[:, n % 2, :], wguh[:, e % 2, fcols], wgul[:, e % 2, fcols], x3h[:, cols],
                            x3l[:, cols], True, True).then_inc(gate_mm, 1)
                    if fc == 0:
                        pe.wait_ge(xel_ready, k + 1)
                    if n >= 2:
                        pe.wait_ge(ha_ready, n - 1)
                    ucols = slice(F + fc * P, F + (fc + 1) * P)
                    product(up_ps[:, n % 2, :], wguh[:, e % 2, ucols], wgul[:, e % 2, ucols], xeh[:, k % 2, :],
                            xel[:, k % 2, :], True, True).then_inc(up_mm, 1)
                    if n >= DOWN_LAG:
                        down(n - DOWN_LAG)
                for n in range(NS - DOWN_LAG, NS):
                    down(n)
                for b in range(NB):
                    pe.wait_ge(acc_done, (E - 1) * GROUPS + b + 1)
                    if b == 0:
                        pe.wait_ge(*after_bank_read(in_bank, LB))
                    if b >= 2:
                        pe.wait_ge(out_ready, b - 1)
                    for t in range(TPB):
                        last = nc.tensor.transpose(turn_ps[b % 2][:, t * P:(t + 1) * P],
                                                   acc[:, b * S + t * P:b * S + (t + 1) * P], ident[:, :])
                    last.then_inc(acc_turned, 1)


def constants():
    import numpy as np

    eye = np.eye(P, dtype=np.float32)
    head_rows = np.zeros((P, UP, P), np.float32)
    for i in range(UH):
        head_rows[32 * (i % 4) + i // 4, i // 2, DH * (i % 2):DH * (i % 2) + DH] = 1.0
    sum_rows = np.ones((P, 2, 32), np.float32)
    sum_rows[:, 0, 1] = 0.0
    sum_rows[:, 1, 0] = 0.0
    lower = np.ascontiguousarray(np.broadcast_to(np.tril(np.ones((8, 8), np.float32), -1), (P, 8, 8)))
    return {"eye": eye, "head_rows": head_rows, "sum_rows": sum_rows, "lower": lower}


def kernel(**inputs):
    import numpy as _np
    import concourse.bacc as _bacc
    from concourse import mybir as _mybir
    from concourse.bass_utils import run_bass_kernel_spmd as _run

    def plain(name):
        return _np.ascontiguousarray(inputs[name])

    def turned(name, *axes):
        return _np.ascontiguousarray(_np.transpose(_np.asarray(inputs[name]), axes))

    data = {
        "x": plain("L0_attn_x"), "ln1_g": plain("L0_attn_ln1_g"), "ln1_b": plain("L0_attn_ln1_b"),
        "wq": plain("L0_attn_Wq"), "wkv": plain("L0_attn_Wkv"), "wo": plain("L0_attn_Wo"),
        "ln2_g": plain("L0_attn_ln2_g"), "ln2_b": plain("L0_attn_ln2_b"),
        "gate_wT": turned("L0_ffn_gate_w", 1, 0), "gate_upT": turned("L0_ffn_gate_up_w", 0, 2, 1),
        "downT": turned("L0_ffn_down_w", 0, 2, 1), **constants(),
    }
    nc = _bacc.Bacc("TRN2", target_bir_lowering=False, num_devices=1)
    arrays, args = {}, []
    for name, a in data.items():
        arrays[f"in_{name}"] = a
        args.append(nc.dram_tensor(f"in_{name}", a.shape, _mybir.dt.from_np(a.dtype), kind="ExternalInput").ap())
    out = nc.dram_tensor("out_0", data["x"].shape, F32, kind="ExternalOutput").ap()
    bass_preln_mqa_moe_kernel(nc, *args, out)
    r = _run(nc, [arrays], core_ids=[0])
    return r.results[0]["out_0"]
```

```python
from contextlib import ExitStack

import concourse.bass as bass
from concourse import mybir

F32 = mybir.dt.float32
F32R = mybir.dt.float32r
ALU = mybir.AluOpType
ACT = mybir.ActivationFunctionType
AX_X = mybir.AxisListType.X

P = 128
HEADS = 16
DH = 64
EPS = 1e-5
UH = 8
UP = UH // 2
JT = 4
TOP_K = 2
Q_SLOTS = 12
SUM_SLOTS = 6
RAW_SLOTS = 5


def attention_schedule(units):
    slots, lead = UH * JT, MAX_LEAD
    placed = []

    def place(slot, order, kind, u, a):
        placed.append((slot, order, (kind, u, a)))

    for n, kind in enumerate(IN_STEPS):
        place(FIRST_V_AT if kind in ("V", "VC") else -1000 + n, 4, kind, 0, 0)
        for b in range(1, units // 2):
            place(2 * slots * (b - 1) + IN_AT[n] + (LATER if b == 1 else 0), 4, kind, b, 0)
    for n, kind in enumerate(AFTER_STEPS):
        for b in range(units // 2 - 1):
            at = AFTER_AT if b < units // 2 - 2 else LATE_AFTER_AT
            place(2 * slots * (b + 1) + at[n], 4, kind, b, 0)
    for pair in range(units * UP):
        u, p = divmod(pair, UP)
        at = (-30, -13, *FIRST_Q_AT)[pair] if pair < 4 else 8 * pair - 19 - lead
        place(at, 3, "Q", u, p)
        place(at + 1, 3, "QHI", u, p)
        place(at + 1, 4, "QLO", u, p)
        for jt in range(JT):
            place(8 * pair + PV_AT[jt], 2, "PV", u, p * JT + jt)
        place(8 * pair + PV_AT[-1] + 1, 1, "RAW", u, p)
    for n in range(units * slots):
        u, a = divmod(n, slots)
        place(n, 0, "EXP", u, a)
        place(n - 15 if n < 12 else (n - 12) // 2 if n < 32 else n - 16 - lead, 1, "MAX", u, a)
    for n, (head, _) in enumerate(shifts(units)):
        place(FIRST_SHIFT_AT[n] if n < 2 else JT * head - lead + 1, 3, "SHIFT", n, 0)
    for u in range(units):
        after = slots * (u + 1)
        if u < units - 1:
            place(after + SUM_AT[0], 5, "SUM", u, 0)
            place(after + SUM_AT[1], 5, "SUM", u, 1)
            place(after + RECIP_AT[4], 5, "RSPLIT", u, 0)
            for c in range(UP):
                place(after + RECIP_AT[c], 5, "RECIP", u, c)
                place(after + NORM_AT[c], 5, "NORM", u, c)
                place(after + NORM_AT[c] + 1, 5, "HIGH", u, c)
                place(after + NORM_AT[c] + 2, 5, "LOW", u, c)
                place(after + NORM_AT[c] + OUT_LAG, 5, "OUT", u, c)
        else:
            for half, start in enumerate((after + HALF_AT[0], after + HALF_AT[1])):
                place(start, 6, "SUM", u, half)
                for c in range(4):
                    place(start + 1 + c, 6, "RECIP", u, 4 * half + c)
                place(start + 5, 6, "RSPLIT", u, half)
                for c in range(2):
                    pair = 2 * half + c
                    place(start + 6 + c, 8, "NORM", u, pair)
                    place(start + 7 + c, 6, "HIGH", u, pair)
                    place(start + 7 + c, 7, "LOW", u, pair)
                    place(max(start + 8 + c, after + HALF_AT[1]), 9, "OUT", u, pair)
    for b in range(units // 2 - 1):
        place(slots * units + XSPLIT_AT[b], 9, "XSPLIT", b, 0)
    place(slots * units - 16, 9, "WSPLIT", 0, 0)
    return [step for _, _, step in sorted(placed, key=lambda entry: entry[:2])]


MAX_LEAD = 6
IN_STEPS = ("STAT0", "APPLY0", "STAT1", "APPLY1", "XT", "XL", "K", "KL", "V", "VC")
IN_AT = (-1, 4, 5, 14, 18, 18, 21, 22, 25, 26)
AFTER_AT = (29, 30, 33, 43, 51, 52, 54, 54, 55, 57, 58, 60, 62)
LATE_AFTER_AT = (29, 30, 33, 41, 44, 46, 47, 48, 49, 50, 52, 54, 56)
EXPERT_AFTER_AT = (0, 0, 2, 5, 7, 9, 10, 10, 10, 12, 12, 14, 16)
PV_AT = (6, 8, 9, 11)
NORM_AT = (14, 17, 19, 22)
OUT_LAG = 5
RECIP_AT = (6, 7, 8, 10, 12)
SUM_AT = (-7, 5)
HALF_AT = (-9, 0)
XSPLIT_AT = (-15, -9, -9)
FIRST_Q_AT = (-3, 3)
FIRST_SHIFT_AT = (-6, 2)
FIRST_V_AT = 5
LATER = 8
VECTOR_HEADS = (3, 5, 7)


def shifts(units):
    return [(0, 2), (2, 2)] + [(head, 4) for head in range(4, units * UH, 4)]


def expert_groups(experts, batches):
    last = batches - 1
    first = [(0, g) for g in range(last)] + [(1, g) for g in range(last - 1)]
    first += [(0, last), (1, last - 1), (1, last)]
    return first + [(e, g) for e in range(2, experts) for g in range(batches)]


AFTER_STEPS = ("YT", "YSTAT", "YADD", "XSTAT", "XNORM", "X3T", "LOGIT", "CHOOSE0", "CHOOSE1", "CHOOSE2",
               "CHOOSE3", "CHOOSE4", "ROWS")


def bass_preln_mqa_moe_kernel(nc, x, ln1_g, ln1_b, wq, wkv, wo, ln2_g, ln2_b, gate_wT, gate_upT, downT,
                              eye, head_rows, sum_rows, low_parts, lower, out):
    NB, S, D = x.shape
    T = NB * S
    TPB = S // P
    E = gate_wT.shape[1]
    F = gate_upT.shape[2] // 2
    FC = F // P
    UNITS = NB * HEADS // UH
    PAIRS = HEADS // 2
    SCALE = float(DH) ** -0.5
    assert D == P and S == 4 * P and JT == TPB and UNITS == 2 * NB

    x_t = x.rearrange("b (t p) d -> b p t d", p=P)
    out_t = out.rearrange("b (t p) d -> b p t d", p=P)
    combine_rows = nc.dram_tensor("combine_rows", [E, T], F32).ap()
    steps = attention_schedule(UNITS)
    shift_heads = shifts(UNITS)
    first_heads = [head for head, _ in shift_heads]
    groups = expert_groups(E, NB)
    last_unit = UNITS - 1

    with ExitStack() as whole:
        def sb(stack, name, shape, dt=F32):
            return stack.enter_context(nc.sbuf_tensor(name, shape, dt))

        def ps(stack, name, shape):
            return stack.enter_context(nc.psum_tensor(name, shape, F32))

        def sem(name):
            return whole.enter_context(nc.semaphore(name))

        ident = sb(whole, "ident", [P, P])
        minus_half = sb(whole, "minus_half", [P, TPB])
        stats = sb(whole, "stats", [P, TPB, 6])
        moments = sb(whole, "moments", [P, TPB, 2])
        var_eps = sb(whole, "var_eps", [P, TPB])
        rstd = sb(whole, "rstd", [P, TPB])
        x1 = sb(whole, "x1", [P, NB * TPB, P])
        yT = sb(whole, "yT", [P, S])
        z = sb(whole, "z", [P, TPB, P])
        x3 = sb(whole, "x3", [P, TPB, P])
        x3T = sb(whole, "x3T", [P, T])
        g2 = sb(whole, "g2", [P, P])
        b2 = sb(whole, "b2", [P, P])
        gw = sb(whole, "gw", [P, E])
        tri = sb(whole, "tri", [P, E, E])
        most = sb(whole, "most", [P, TPB])
        over = sb(whole, "over", [P, TPB])
        pr = sb(whole, "pr", [P, TPB, E])
        cmp = sb(whole, "cmp", [P, TPB, E, E])
        eqs = sb(whole, "eqs", [P, TPB, E, E])
        cnt = sb(whole, "cnt", [P, TPB, E])
        comb = sb(whole, "comb", [P, TPB, E])
        combT = sb(whole, "combT", [E, S])
        wgu_raw = sb(whole, "wgu_raw", [P, 2, 2 * F])
        wdn_raw = sb(whole, "wdn_raw", [P, 2, FC, P])

        xh = sb(whole, "xh", [P, 2, S], F32R)
        xl = sb(whole, "xl", [P, 2, S], F32R)
        wqh = sb(whole, "wqh", [P, HEADS * DH], F32R)
        wql = sb(whole, "wql", [P, HEADS * DH], F32R)
        q_hl = sb(whole, "q_hl", [P, Q_SLOTS, S], F32R)
        q_hm = sb(whole, "q_hm", [P, Q_SLOTS, S], F32R)
        wguh, wgul = [wqh], [wql]
        wdnh, wdnl = ([part[:, 0, :].rearrange("p (c n) -> p c n", n=P)] for part in (xh, xl))
        assert (UNITS * UH - 4) % Q_SLOTS == 0 and 2 * F == HEADS * DH and (NB - 1) % 2 == 1
        cb = q_hl[:, 4:8, :].bitcast(F32)
        x3h = q_hm[:, 4:8, :].rearrange("p g s -> p (g s)")
        x3l = q_hm[:, 8:12, :].rearrange("p g s -> p (g s)")

        half_set = sem("half_set")
        x1_in = [sem(f"x1_in{b}") for b in range(NB)]
        consts_in = sem("consts_in")
        consts2_in = sem("consts2_in")
        ln_stats = sem("ln_stats")
        ln_rstd = sem("ln_rstd")
        dve_own = sem("dve_own")
        pool_own = sem("pool_own")
        y_ready = sem("y_ready")
        y_turned = sem("y_turned")
        z_ready = sem("z_ready")
        y_normed = sem("y_normed")
        y_added = sem("y_added")
        x3_ready = sem("x3_ready")
        x3_turned = sem("x3_turned")
        x3T_ready = sem("x3T_ready")
        logit_mm = sem("logit_mm")
        logit_less = sem("logit_less")
        prob_exp = sem("prob_exp")
        comb_ready = sem("comb_ready")
        comb_turned = sem("comb_turned")
        combT_ready = sem("combT_ready")
        rows_out = sem("rows_out")
        gu_in = [sem(f"gu_in{n}") for n in range(2)]
        dn_in = [sem(f"dn_in{n}") for n in range(2)]
        cb_in = [sem(f"cb_in{n}") for n in range(4)]
        w_split = sem("w_split")
        x3h_ready = sem("x3h_ready")
        x3l_ready = sem("x3l_ready")
        count = {"dve": 0, "pool": 0, "ln": 0, "ln_pool": 0}

        def link(dve, ins):
            ins.then_inc(dve_own, 1)
            count["dve"] += 1
            dve.wait_ge(dve_own, count["dve"])

        def link_pool(pool, ins):
            ins.then_inc(pool_own, 1)
            count["pool"] += 1
            pool.wait_ge(pool_own, count["pool"])

        def ln_moments(dve, tile):
            for t in range(TPB):
                last = nc.vector.bn_stats(stats[:, t, :], tile[:, t, :])
            link(dve, last)
            for t in range(TPB):
                last = nc.vector.bn_aggr(moments[:, t, :], stats[:, t, :])
            last.then_inc(ln_stats, 1)

        def ln_rsqrt(pool):
            count["ln_pool"] += 1
            pool.wait_ge(ln_stats, count["ln_pool"])
            link_pool(pool, nc.gpsimd.tensor_scalar(var_eps[:, :], moments[:, :, 1], 1.0, EPS, ALU.mult, ALU.add))
            nc.gpsimd.tensor_tensor(rstd[:, :], var_eps[:, :], minus_half[:, :], ALU.pow).then_inc(ln_rstd, 1)

        def ln_apply(dve, dst, src):
            count["ln"] += 1
            dve.wait_ge(ln_rstd, count["ln"])
            for t in range(TPB):
                last = nc.vector.tensor_scalar(dst[:, t, :], src[:, t, :], moments[:, t, 0:1], rstd[:, t:t + 1],
                                               ALU.subtract, ALU.mult)
            return last

        def after_bank_read(kind, b):
            return {"YT": (z_ready, b + 1), "X3T": (x3T_ready, b + 1), "LOGIT": (logit_less, b + 1),
                    "ROWS": (combT_ready, b + 1)}[kind]

        def after_tensor(pe, kind, b, bank):
            if kind == "YT":
                pe.wait_ge(y_ready, b + 1)
                for t in range(TPB):
                    last = nc.tensor.transpose(bank[:, t * P:(t + 1) * P], yT[:, t * P:(t + 1) * P], ident[:, :])
                last.then_inc(y_turned, 1)
            if kind == "X3T":
                pe.wait_ge(x3_ready, b + 1)
                for t in range(TPB):
                    last = nc.tensor.transpose(bank[:, t * P:(t + 1) * P], x3[:, t, :], ident[:, :])
                last.then_inc(x3_turned, 1)
            if kind == "LOGIT":
                pe.wait_ge(x3T_ready, b + 1)
                if b == 0:
                    pe.wait_ge(consts2_in, 64)
                for t in range(TPB):
                    last = nc.tensor.matmul(bank[:, t * E:(t + 1) * E], x3T[:, b * S + t * P:b * S + (t + 1) * P],
                                            gw[:, :], start=True, stop=True)
                last.then_inc(logit_mm, 1)
            if kind == "ROWS":
                pe.wait_ge(comb_ready, b + 1)
                for t in range(TPB):
                    last = nc.tensor.transpose(bank[0:E, t * P:(t + 1) * P], comb[:, t, :], ident[:, :])
                last.then_inc(comb_turned, 1)

        def after_scalar(act, kind, b, bank):
            if kind == "YT":
                act.wait_ge(y_turned, b + 1)
                nc.scalar.activation(z[:, :, :], bank[:, :].rearrange("p (t d) -> p t d", d=P),
                                     ACT.Copy).then_inc(z_ready, 1)
            if kind == "X3T":
                act.wait_ge(x3_turned, b + 1)
                nc.scalar.activation(x3T[:, b * S:(b + 1) * S], bank[:, :], ACT.Copy).then_inc(x3T_ready, 1)
            if kind == "CHOOSE0":
                act.wait_ge(logit_less, b + 1)
                nc.scalar.activation(pr[:, :, :], pr[:, :, :], ACT.Exp).then_inc(prob_exp, 1)
            if kind == "ROWS":
                act.wait_ge(comb_turned, b + 1)
                if b >= 1:
                    act.wait_ge(rows_out, 16 * b)
                nc.scalar.activation(combT[:, :], bank[0:E, :], ACT.Copy).then_inc(combT_ready, 1)

        def after_gpsimd(pool, kind, b):
            if kind in ("YSTAT", "XSTAT"):
                ln_rsqrt(pool)
            if kind == "YADD":
                pool.wait_ge(y_normed, b + 1)
                if b == 0:
                    pool.wait_ge(consts2_in, 64)
                tiles = x1[:, b * TPB:(b + 1) * TPB, :]
                link_pool(pool, nc.gpsimd.tensor_tensor(z[:, :, :], z[:, :, :],
                                                        g2[:, :].unsqueeze(1).broadcast_to([P, TPB, P]), ALU.mult))
                link_pool(pool, nc.gpsimd.tensor_tensor(z[:, :, :], z[:, :, :],
                                                        b2[:, :].unsqueeze(1).broadcast_to([P, TPB, P]), ALU.add))
                nc.gpsimd.tensor_tensor(tiles, tiles, z[:, :, :], ALU.add).then_inc(y_added, 1)

        def after_vector(dve, kind, b, bank):
            tiles = x1[:, b * TPB:(b + 1) * TPB, :]
            if kind == "YSTAT":
                dve.wait_ge(z_ready, b + 1)
                ln_moments(dve, z)
            if kind == "YADD":
                ln_apply(dve, z, z).then_inc(y_normed, 1)
            if kind == "XSTAT":
                dve.wait_ge(y_added, b + 1)
                ln_moments(dve, tiles)
            if kind == "XNORM":
                if b >= 1:
                    dve.wait_ge(x3_turned, b)
                ln_apply(dve, x3, tiles).then_inc(x3_ready, 1)
            if kind == "CHOOSE0":
                logits = bank[:, 0:TPB * E].rearrange("p (t e) -> p t e", e=E)
                dve.wait_ge(logit_mm, b + 1)
                link(dve, nc.vector.tensor_reduce(most[:, :], logits, AX_X, ALU.max))
                nc.vector.tensor_tensor(pr[:, :, :], logits, most[:, :].unsqueeze(2).broadcast_to([P, TPB, E]),
                                        ALU.subtract).then_inc(logit_less, 1)
            if kind == "CHOOSE1":
                dve.wait_ge(prob_exp, b + 1)
                link(dve, nc.vector.tensor_reduce(most[:, :], pr[:, :, :], AX_X, ALU.add))
                link(dve, nc.vector.reciprocal(over[:, :], most[:, :]))
                link(dve, nc.vector.tensor_tensor(pr[:, :, :], pr[:, :, :],
                                                  over[:, :].unsqueeze(2).broadcast_to([P, TPB, E]), ALU.mult))
            if kind == "CHOOSE2":
                other = pr[:, :, :].unsqueeze(2).broadcast_to([P, TPB, E, E])
                this = pr[:, :, :].unsqueeze(3).broadcast_to([P, TPB, E, E])
                nc.vector.tensor_tensor(cmp[:, :, :, :], other, this, ALU.is_gt)
                link(dve, nc.vector.tensor_tensor(eqs[:, :, :, :], other, this, ALU.is_equal))
                link(dve, nc.vector.tensor_tensor(eqs[:, :, :, :], eqs[:, :, :, :],
                                                  tri[:, :, :].unsqueeze(1).broadcast_to([P, TPB, E, E]), ALU.mult))
            if kind == "CHOOSE3":
                link(dve, nc.vector.tensor_tensor(cmp[:, :, :, :], cmp[:, :, :, :], eqs[:, :, :, :], ALU.add))
                link(dve, nc.vector.tensor_reduce(cnt[:, :, :], cmp[:, :, :, :], AX_X, ALU.add))
            if kind == "CHOOSE4":
                link(dve, nc.vector.tensor_scalar(cnt[:, :, :], cnt[:, :, :], TOP_K - 0.5, None, ALU.is_lt))
                link(dve, nc.vector.tensor_tensor(pr[:, :, :], pr[:, :, :], cnt[:, :, :], ALU.mult))
                link(dve, nc.vector.tensor_reduce(most[:, :], pr[:, :, :], AX_X, ALU.add))
                link(dve, nc.vector.reciprocal(over[:, :], most[:, :]))
                if b >= 1:
                    dve.wait_ge(comb_turned, b)
                nc.vector.tensor_tensor(comb[:, :, :], pr[:, :, :],
                                        over[:, :].unsqueeze(2).broadcast_to([P, TPB, E]),
                                        ALU.mult).then_inc(comb_ready, 1)

        def load_expert(sp, e):
            sp.dma_start(wgu_raw[:, e % 2, :], gate_upT[e]).then_inc(gu_in[e % 2], 16)
            sp.dma_start(wdn_raw[:, e % 2, :, :],
                         downT[e].rearrange("(c p) n -> p c n", p=P)).then_inc(dn_in[e % 2], 16)

        def load_combine(sp, k):
            e, g = groups[k]
            sp.dma_start(cb[:, k % 4, :],
                         combine_rows[e, g * S:(g + 1) * S].partition_broadcast(P)).then_inc(cb_in[k % 4], 16)

        def x_high(act, g):
            nc.scalar.activation(x3h[:, g * S:(g + 1) * S], x3T[:, g * S:(g + 1) * S], ACT.Copy).then_inc(x3h_ready, 1)

        def x_low(dve, g):
            dve.wait_ge(x3h_ready, g + 1)
            nc.vector.tensor_tensor(x3l[:, g * S:(g + 1) * S], x3T[:, g * S:(g + 1) * S],
                                    x3h[:, g * S:(g + 1) * S].bitcast(F32), ALU.subtract).then_inc(x3l_ready, 1)

        def split_weights(pool, e):
            for raw_in, raw_ap, high, low in ((gu_in, wgu_raw[:, e % 2, :], wguh[e % 2][:, :], wgul[e % 2][:, :]),
                                              (dn_in, wdn_raw[:, e % 2, :, :], wdnh[e % 2][:, :, :],
                                               wdnl[e % 2][:, :, :])):
                pool.wait_ge(raw_in[e % 2], 16 * (e // 2 + 1))
                link_pool(pool, nc.gpsimd.tensor_scalar(high, raw_ap, 1.0, 1.0, ALU.mult, ALU.mult))
                nc.gpsimd.tensor_tensor(low, raw_ap, high.bitcast(F32), ALU.subtract).then_inc(w_split, 1)

        def after_sync(sp, kind, b):
            if kind == "ROWS":
                sp.wait_ge(combT_ready, b + 1)
                sp.dma_start(combine_rows[:, b * S:(b + 1) * S], combT[:, :]).then_inc(rows_out, 16)

        with ExitStack() as att:
            gcol = sb(att, "gcol", [P, 1])
            bcol = sb(att, "bcol", [P, 1])
            xn = x3
            xnT = z[:, :, :].rearrange("p t d -> p (t d)")
            khh = sb(att, "khh", [P, 2, S], F32R)
            kly = sb(att, "kly", [P, 2, S], F32R)
            v = sb(att, "v", [P, 2, TPB, DH])
            wkh = sb(att, "wkh", [P, P], F32R)
            wkl = sb(att, "wkl", [P, P], F32R)
            wvh = sb(att, "wvh", [P, DH], F32R)
            wvl = sb(att, "wvl", [P, DH], F32R)
            woh = sb(att, "woh", [P, PAIRS, P], F32R)
            wol = sb(att, "wol", [P, PAIRS, P], F32R)
            rowmax = sb(att, "rowmax", [P, 2, TPB, 4])
            mrow = sb(att, "mrow", [4, 2, S], F32R)
            prob = sb(att, "prob", [P, 4, JT, S])
            fold = sb(att, "fold", [P, 2, S])
            psums = sb(att, "psums", [P, SUM_SLOTS, S])
            sumsel = sb(att, "sumsel", [P, 3, 32])
            headsel = sb(att, "headsel", [P, UP, P], F32R)
            rih = sb(att, "rih", [P, S], F32R)
            rhl = sb(att, "rhl", [P, S], F32R)
            low_rows = sb(att, "low_rows", [P, 1])
            raw = sb(att, "raw", [P, RAW_SLOTS, S])
            ao = sb(att, "ao", [P, S])
            rinv = ao
            aoh = sb(att, "aoh", [P, 2, S], F32R)
            aol = sb(att, "aol", [P, 2, S], F32R)
            wq_raw = prob[:, 0, 0:2, :].rearrange("p a s -> p (a s)")
            wo_raw = prob[:, 0, 2:4, :].rearrange("p a (c n) -> p (a c) n", n=P)
            wk_raw = prob[:, 1, 0, 0:P]
            wv_raw = prob[:, 1, 0, P:P + DH]
            hs_raw = prob[:, 1, 1, :].rearrange("p (u n) -> p u n", n=P)

            q_ps = ps(att, "q_ps", [P, S])
            max_ps = ps(att, "max_ps", [P, 2, S])
            s_ps = ps(att, "s_ps", [P, 2, S])
            pv_ps = ps(att, "pv_ps", [P, S])
            sum_ps = ps(att, "sum_ps", [P, S])
            y_ps = ps(att, "y_ps", [P, S])

            names = """wkv_in wq_in wo_in ones_set wkv_split wq_split wo_split headsel_set
                xn_ready x_turned xnT_sb xh_ready xl_ready k_mm kh_ready kl_ready v_mm v_ready
                q_mm q_hi q_lo q_top max_mm max_done shift_mm mrow_ready score_mm exp_done
                pv_mm raw_ready prob_folded head_sum sum_mm recip_done norm_mm ao_ready aoh_ready ao_split
                out_mm""".split()
            (wkv_in, wq_in, wo_in, ones_set, wkv_split, wq_split, wo_split, headsel_set,
             xn_ready, x_turned, xnT_sb, xh_ready, xl_ready, k_mm, kh_ready, kl_ready, v_mm, v_ready,
             q_mm, q_hi, q_lo, q_top, max_mm, max_done, shift_mm, mrow_ready, score_mm, exp_done,
             pv_mm, raw_ready, prob_folded, head_sum, sum_mm, recip_done, norm_mm, ao_ready, aoh_ready, ao_split,
             out_mm) = [sem(n) for n in names]
            mrow_in = [sem(f"mrow_in{n}") for n in range(2)]

            def vector_sums(head):
                return head // UH == last_unit and head % UH in VECTOR_HEADS

            gpsimd_heads = [h for h in range(UNITS * UH) if not vector_sums(h)]
            vector_heads = [h for h in range(UNITS * UH) if vector_sums(h)]
            vec_sum = sem("vec_sum")

            def sums_done(eng, heads):
                eng.wait_ge(head_sum, sum(h < heads for h in gpsimd_heads))
                if any(h < heads for h in vector_heads):
                    eng.wait_ge(vec_sum, sum(h < heads for h in vector_heads))

            def recips(u, pair):
                return u + 1 + (u == last_unit and pair >= 2)

            def k_bank(b):
                return pv_ps if b == 0 else q_ps

            block = att.enter_context(nc.Block())

            @block.sync
            def _(sp):
                sp.dma_start(x1[:, 0:TPB, :], x_t[0]).then_inc(x1_in[0], 16)
                for dst, src in ((ident[:, :], eye), (gcol[:, :], ln1_g.rearrange("(p o) -> p o", o=1)),
                                 (bcol[:, :], ln1_b.rearrange("(p o) -> p o", o=1)),
                                 (hs_raw, head_rows), (sumsel[:, :, :], sum_rows), (low_rows[:, :], low_parts)):
                    sp.dma_start(dst, src).then_inc(consts_in, 16)
                sp.dma_start(wk_raw[:, 0:DH], wkv[:, 0:DH]).then_inc(wkv_in, 16)
                sp.dma_start(wk_raw[:, DH:P], wkv[:, 0:DH]).then_inc(wkv_in, 16)
                sp.dma_start(wv_raw, wkv[:, DH:2 * DH]).then_inc(wkv_in, 16)
                sp.dma_start(wq_raw, wq).then_inc(wq_in, 16)
                sp.dma_start(wo_raw, wo.rearrange("(c p) n -> p c n", p=P)).then_inc(wo_in, 16)
                for b in range(1, NB):
                    sp.dma_start(x1[:, b * TPB:(b + 1) * TPB, :], x_t[b]).then_inc(x1_in[b], 16)
                for dst, src in ((g2[:, :], ln2_g.partition_broadcast(P)), (b2[:, :], ln2_b.partition_broadcast(P)),
                                 (gw[:, :], gate_wT), (tri[:, :, :], lower)):
                    sp.dma_start(dst, src).then_inc(consts2_in, 16)
                for kind, u, a in steps:
                    if kind == "SHIFT":
                        head, heads = shift_heads[u]
                        sp.wait_ge(mrow_ready, 2 * (u + 1))
                        if head >= Q_SLOTS:
                            sp.wait_ge(score_mm, (head + heads - Q_SLOTS) * JT)
                        slot = head % Q_SLOTS
                        for part in range(2):
                            sp.dma_start(q_hm[DH + part:DH + part + 1, slot:slot + heads, :].bitcast(F32),
                                         mrow[0:heads, part, :].bitcast(F32)).then_inc(mrow_in[u % 2], 16)
                    if kind in AFTER_STEPS:
                        after_sync(sp, kind, u)
                    if kind == "V" and u == NB - 1:
                        for e in range(2):
                            load_expert(sp, e)
                sp.wait_ge(rows_out, 16 * (NB - 1))
                sp.wait_ge(score_mm, (UNITS * UH - 4) * JT)
                for k in range(4):
                    load_combine(sp, k)

            @block.gpsimd
            def _(pool):
                nc.gpsimd.memset(minus_half[:, :], -0.5).then_inc(half_set, 1)
                pool.wait_ge(half_set, 1)

                def split(raw_ap, high, low, done):
                    link_pool(pool, nc.gpsimd.tensor_scalar(high, raw_ap, 1.0, 1.0, ALU.mult, ALU.mult))
                    nc.gpsimd.tensor_tensor(low, raw_ap, high.bitcast(F32), ALU.subtract).then_inc(done, 1)

                for kind, u, a in steps:
                    if kind in ("STAT0", "STAT1"):
                        ln_rsqrt(pool)
                    if kind == "STAT1" and u == 0:
                        pool.wait_ge(wkv_in, 48)
                        split(wk_raw, wkh[:, :], wkl[:, :], wkv_split)
                        split(wv_raw, wvh[:, :], wvl[:, :], wkv_split)
                        pool.wait_ge(wq_in, 16)
                        for c in range(2):
                            half = slice(c * S, (c + 1) * S)
                            split(wq_raw[:, half], wqh[:, half], wql[:, half], wq_split)
                    if kind == "Q":
                        k = u * UP + a
                        pool.wait_ge(q_hi, 2 * (k + 1))
                        slots = slice(2 * k % Q_SLOTS, 2 * k % Q_SLOTS + 2)
                        nc.gpsimd.tensor_scalar(q_hm[0:DH, slots, :], q_hl[0:DH, slots, :].bitcast(F32),
                                                1.0, 1.0, ALU.mult, ALU.mult).then_inc(q_top, 1)
                        if k == 0:
                            pool.wait_ge(consts_in, 96)
                            nc.gpsimd.tensor_scalar(headsel[:, :, :], hs_raw, 1.0, 1.0, ALU.mult,
                                                    ALU.mult).then_inc(headsel_set, 1)
                            pool.wait_ge(wo_in, 16)
                            split(wo_raw, woh[:, :, :], wol[:, :, :], wo_split)
                    if kind == "EXP" and a % JT == JT - 1:
                        head = u * UH + a // JT
                        if not vector_sums(head):
                            done = gpsimd_heads.index(head)
                            pool.wait_ge(exp_done, (head + 1) * JT)
                            if done >= 1:
                                pool.wait_ge(head_sum, done)
                            nc.gpsimd.tensor_tensor(fold[:, :, :], prob[:, head % 4, 0:2, :],
                                                    prob[:, head % 4, 2:4, :], ALU.add).then_inc(prob_folded, 1)
                            pool.wait_ge(prob_folded, done + 1)
                            if head >= SUM_SLOTS:
                                pool.wait_ge(sum_mm, (head - SUM_SLOTS) // 4 + 1)
                            nc.gpsimd.tensor_tensor(psums[:, head % SUM_SLOTS, :], fold[:, 0, :], fold[:, 1, :],
                                                    ALU.add).then_inc(head_sum, 1)
                    if kind == "XL" and u >= 1:
                        pool.wait_ge(xh_ready, u + 1)
                        nc.gpsimd.tensor_tensor(xl[:, u % 2, :], xnT[:, :], xh[:, u % 2, :].bitcast(F32),
                                                ALU.subtract).then_inc(xl_ready, 1)
                    if kind in AFTER_STEPS:
                        after_gpsimd(pool, kind, u)
                    if kind == "WSPLIT":
                        pool.wait_ge(q_mm, UNITS * UP)
                        split_weights(pool, 0)

            @block.vector
            def _(dve):
                nc.vector.memset(kly[DH:DH + 2, :, :].bitcast(F32), 1.0).then_inc(ones_set, 1)
                for kind, u, a in steps:
                    b = u
                    if kind == "STAT0":
                        dve.wait_ge(x1_in[b], 16)
                        ln_moments(dve, x1[:, b * TPB:(b + 1) * TPB, :])
                    if kind == "APPLY0":
                        if b >= 1:
                            dve.wait_ge(x_turned, b)
                        link(dve, ln_apply(dve, xn, x1[:, b * TPB:(b + 1) * TPB, :]))
                    if kind == "STAT1":
                        ln_moments(dve, xn)
                    if kind == "APPLY1":
                        ln_apply(dve, xn, xn).then_inc(xn_ready, 1)
                    if kind == "XT":
                        dve.wait_ge(x_turned, b + 1)
                        if b == 0:
                            dve.wait_ge(consts_in, 96)
                        else:
                            dve.wait_ge(xh_ready, b)
                            dve.wait_ge(xl_ready, b)
                        nc.vector.tensor_scalar(xnT[:, :], q_ps[:, :], gcol[:, :], bcol[:, :], ALU.mult,
                                                ALU.add).then_inc(xnT_sb, 1)
                    if kind == "XL" and b == 0:
                        dve.wait_ge(xh_ready, 1)
                        nc.vector.tensor_tensor(xl[:, 0, :], xnT[:, :], xh[:, 0, :].bitcast(F32),
                                                ALU.subtract).then_inc(xl_ready, 1)
                    if kind == "KL":
                        dve.wait_ge(kh_ready, b + 1)
                        nc.vector.tensor_tensor(kly[0:DH, b % 2, :], k_bank(b)[0:DH, :],
                                                khh[0:DH, b % 2, :].bitcast(F32),
                                                ALU.subtract).then_inc(kl_ready, 1)
                    if kind == "QLO":
                        for hd in range(2):
                            h = 2 * (u * UP + a) + hd
                            dve.wait_ge(q_hi, h + 1)
                            nc.vector.tensor_tensor(q_hl[DH:P, h % Q_SLOTS, :], q_ps[DH * hd:DH * hd + DH, :],
                                                    q_hl[0:DH, h % Q_SLOTS, :].bitcast(F32),
                                                    ALU.subtract).then_inc(q_lo, 1)
                    if kind == "MAX":
                        k = u * UH * JT + a
                        head, it = divmod(k, JT)
                        group, i = divmod(head, 4)
                        dve.wait_ge(max_mm, k + 1)
                        if i == 0 and it == 0 and group >= 2:
                            dve.wait_ge(shift_mm, group)
                        nc.vector.tensor_reduce(rowmax[:, group % 2, it, i:i + 1], max_ps[:, k % 2, :], AX_X,
                                                ALU.max).then_inc(max_done, 1)
                    if kind == "SHIFT":
                        heads = shift_heads[u][1]
                        dve.wait_ge(mrow_ready, 2 * u + 1)
                        nc.vector.scalar_tensor_tensor(out=mrow[0:heads, 1, :], in0=q_ps[0:heads, :], scalar=-1.0,
                                                       in1=mrow[0:heads, 0, :].bitcast(F32), op0=ALU.mult,
                                                       op1=ALU.subtract).then_inc(mrow_ready, 1)
                    if kind == "EXP" and a % JT == JT - 1 and vector_sums(u * UH + a // JT):
                        head = u * UH + a // JT
                        dve.wait_ge(exp_done, (head + 1) * JT)
                        dve.wait_ge(sum_mm, (head - SUM_SLOTS) // 4 + 1)
                        nc.vector.tensor_reduce(psums[:, head % SUM_SLOTS, :],
                                                prob[:, head % 4, :, :].rearrange("p j s -> p s j"), AX_X,
                                                ALU.add).then_inc(vec_sum, 1)
                    if kind == "RECIP":
                        half, n = divmod(a, 4)
                        quarter = slice(n * P, (n + 1) * P)
                        if n == 0:
                            dve.wait_ge(sum_mm, 2 * u + half + 1 if u == last_unit else 2 * (u + 1))
                            if u >= 1:
                                dve.wait_ge(ao_split, u * UP + 2 * half)
                        last = nc.vector.reciprocal(rinv[:, quarter], sum_ps[:, quarter])
                        if n == 3:
                            link(dve, last)
                    if kind == "RSPLIT":
                        if u >= 1:
                            dve.wait_ge(norm_mm, u * UP + 2 * a)
                        link(dve, nc.vector.tensor_copy(rih[:, :], rinv[:, :]))
                        nc.vector.scalar_tensor_tensor(out=rhl[:, :], in0=rih[:, :].bitcast(F32),
                                                       scalar=low_rows[:, 0:1], in1=rinv[:, :], op0=ALU.mult,
                                                       op1=ALU.add).then_inc(recip_done, 1)
                    if kind == "NORM":
                        k = u * UP + a
                        dve.wait_ge(norm_mm, k + 1)
                        dve.wait_ge(raw_ready, k + 1)
                        if a >= 1:
                            dve.wait_ge(ao_split, k)
                        dve.wait_ge(recip_done, recips(u, a))
                        nc.vector.tensor_tensor(ao[:, :], sum_ps[:, :], raw[:, k % RAW_SLOTS, :],
                                                ALU.mult).then_inc(ao_ready, 1)
                    if kind == "LOW":
                        k = u * UP + a
                        dve.wait_ge(aoh_ready, k + 1)
                        nc.vector.tensor_tensor(aol[:, k % 2, :], ao[:, :], aoh[:, k % 2, :].bitcast(F32),
                                                ALU.subtract).then_inc(ao_split, 1)
                    if kind == "XSPLIT":
                        x_low(dve, b)
                    if kind in AFTER_STEPS:
                        after_vector(dve, kind, b, q_ps)

            @block.scalar
            def _(act):
                for kind, u, a in steps:
                    b = u
                    if kind == "XT":
                        act.wait_ge(xnT_sb, b + 1)
                        if b >= 2:
                            act.wait_ge(q_mm, (b - 1) * PAIRS)
                        nc.scalar.activation(xh[:, b % 2, :], xnT[:, :], ACT.Copy).then_inc(xh_ready, 1)
                    if kind == "K":
                        act.wait_ge(k_mm, b + 1)
                        nc.scalar.activation(khh[:, b % 2, :], k_bank(b)[:, :], ACT.Copy).then_inc(kh_ready, 1)
                    if kind == "VC":
                        act.wait_ge(v_mm, b + 1)
                        nc.scalar.activation(v[:, b % 2, :, :], q_ps[:, 0:TPB * DH].rearrange("p (t d) -> p t d", d=DH),
                                             ACT.Copy).then_inc(v_ready, 1)
                    if kind == "SHIFT":
                        heads = shift_heads[u][1]
                        act.wait_ge(shift_mm, u + 1)
                        if u >= 1:
                            act.wait_ge(mrow_in[(u - 1) % 2], 32 * ((u - 1) // 2 + 1))
                        nc.scalar.activation(mrow[0:heads, 0, :], q_ps[0:heads, :], ACT.Copy,
                                             scale=-1.0).then_inc(mrow_ready, 1)
                    if kind == "QHI":
                        k = u * UP + a
                        act.wait_ge(q_mm, k + 1)
                        if 2 * k >= Q_SLOTS:
                            act.wait_ge(score_mm, (2 * k + 2 - Q_SLOTS) * JT)
                        for hd in range(2):
                            nc.scalar.activation(q_hl[0:DH, (2 * k + hd) % Q_SLOTS, :], q_ps[DH * hd:DH * hd + DH, :],
                                                 ACT.Copy).then_inc(q_hi, 1)
                    if kind == "EXP":
                        k = u * UH * JT + a
                        head, jt = divmod(k, JT)
                        act.wait_ge(score_mm, k + 1)
                        if k == 0:
                            act.wait_ge(wkv_split, 2)
                            act.wait_ge(wq_split, 2)
                            act.wait_ge(headsel_set, 1)
                            act.wait_ge(wo_split, 1)
                        elif head >= 4 and jt == 0:
                            act.wait_ge(pv_mm, (head - 4) // 2 + 1)
                            if vector_sums(head - 4):
                                act.wait_ge(vec_sum, vector_heads.index(head - 4) + 1)
                            else:
                                act.wait_ge(prob_folded, gpsimd_heads.index(head - 4) + 1)
                        nc.scalar.activation(prob[:, head % 4, jt, :], s_ps[:, k % 2, :], ACT.Exp,
                                             scale=SCALE).then_inc(exp_done, 1)
                    if kind == "RAW":
                        k = u * UP + a
                        act.wait_ge(pv_mm, k + 1)
                        if k >= RAW_SLOTS:
                            act.wait_ge(ao_ready, k - RAW_SLOTS + 1)
                        nc.scalar.activation(raw[:, k % RAW_SLOTS, :], pv_ps[:, :], ACT.Copy).then_inc(raw_ready, 1)
                    if kind == "HIGH":
                        k = u * UP + a
                        act.wait_ge(ao_ready, k + 1)
                        if k >= 2:
                            act.wait_ge(out_mm, k - 1)
                        nc.scalar.activation(aoh[:, k % 2, :], ao[:, :], ACT.Copy).then_inc(aoh_ready, 1)
                    if kind == "OUT" and (u * UP + a) % PAIRS == PAIRS - 1:
                        b = (u * UP + a) // PAIRS
                        act.wait_ge(out_mm, PAIRS * (b + 1))
                        if b >= 1:
                            act.wait_ge(y_turned, b)
                        nc.scalar.activation(yT[:, :], y_ps[:, :], ACT.Copy).then_inc(y_ready, 1)
                    if kind == "XSPLIT":
                        act.wait_ge(score_mm, (UNITS * UH - 4) * JT)
                        act.wait_ge(x3T_ready, b + 1)
                        x_high(act, b)
                    if kind in AFTER_STEPS:
                        after_scalar(act, kind, b, q_ps)

            @block.tensor
            def _(pe):
                def product(dst, wh, wl, mh, ml, start, stop):
                    nc.tensor.matmul(dst, wh, mh, start=start, stop=False, skip_group_check=True)
                    nc.tensor.matmul(dst, wl, mh, start=False, stop=False, skip_group_check=True)
                    return nc.tensor.matmul(dst, wh, ml, start=False, stop=stop, skip_group_check=True)

                def bank_read(kind, u, a):
                    if kind in AFTER_STEPS:
                        return after_bank_read(kind, u)
                    return {"XT": (xnT_sb, u + 1), "K": (kl_ready, u + 1), "V": (v_ready, u + 1),
                            "Q": (q_lo, 2 * (u * UP + a + 1)), "SHIFT": (mrow_ready, 2 * (u + 1))}[kind]

                pe.wait_ge(consts_in, 96)
                in_bank = None
                for kind, u, a in steps:
                    b = u // 2
                    if kind in ("XT", "K", "V", "Q", "SHIFT", "YT", "X3T", "LOGIT", "ROWS") and (kind, u) != ("K", 0):
                        if in_bank:
                            pe.wait_ge(*bank_read(*in_bank))
                        in_bank = (kind, u, a)
                    if kind == "XT":
                        pe.wait_ge(xn_ready, u + 1)
                        for t in range(TPB):
                            last = nc.tensor.transpose(q_ps[:, t * P:(t + 1) * P], xn[:, t, :], ident[:, :])
                        last.then_inc(x_turned, 1)
                    if kind == "K":
                        pe.wait_ge(xl_ready, u + 1)
                        if u == 0:
                            pe.wait_ge(wkv_split, 2)
                        product(k_bank(u)[:, :], wkh[:, :], wkl[:, :], xh[:, u % 2, :], xl[:, u % 2, :],
                                True, True).then_inc(k_mm, 1)
                    if kind == "V":
                        for t in range(TPB):
                            tile = slice(t * P, (t + 1) * P)
                            last = product(q_ps[:, t * DH:(t + 1) * DH], xh[:, u % 2, tile], xl[:, u % 2, tile],
                                           wvh[:, :], wvl[:, :], t == 0, t == TPB - 1)
                        last.then_inc(v_mm, 1)
                    if kind == "Q":
                        c = (u * UP + a) % PAIRS
                        if u == 0 and a == 0:
                            pe.wait_ge(wq_split, 2)
                            pe.wait_ge(xl_ready, 1)
                        wcols = slice(c * P, (c + 1) * P)
                        product(q_ps[:, :], wqh[:, wcols], wql[:, wcols], xh[:, b % 2, :], xl[:, b % 2, :],
                                True, True).then_inc(q_mm, 1)
                    if kind == "MAX":
                        i, it = divmod(a, JT)
                        k = u * UH * JT + a
                        if it == 0:
                            pe.wait_ge(q_lo, u * UH + i + 1)
                        if k >= 2:
                            pe.wait_ge(max_done, k - 1)
                        nc.tensor.matmul(max_ps[:, k % 2, :], q_hl[:, k // JT % Q_SLOTS, it * P:(it + 1) * P],
                                         khh[:, b % 2, :], start=True, stop=True).then_inc(max_mm, 1)
                    if kind == "SHIFT":
                        head, heads = shift_heads[u]
                        pe.wait_ge(max_done, (head + heads) * JT)
                        group, i = divmod(head, 4)
                        for t in range(TPB):
                            last = nc.tensor.transpose(q_ps[0:heads, t * P:(t + 1) * P],
                                                       rowmax[:, group % 2, t, i:i + heads],
                                                       ident[:, :])
                        last.then_inc(shift_mm, 1)
                    if kind == "EXP":
                        k = u * UH * JT + a
                        i, jt = divmod(a, JT)
                        if k == 0:
                            pe.wait_ge(ones_set, 1)
                        if a == 0 and u % 2 == 0:
                            pe.wait_ge(kl_ready, b + 1)
                        if jt == 0 and k // JT in first_heads:
                            n = first_heads.index(k // JT)
                            pe.wait_ge(mrow_in[n % 2], 32 * (n // 2 + 1))
                        if a % (2 * JT) == 0:
                            pe.wait_ge(q_top, u * UP + i // 2 + 1)
                        if k >= 2:
                            pe.wait_ge(exp_done, k - 1)
                        keys = slice(jt * P, (jt + 1) * P)
                        slot = k // JT % Q_SLOTS
                        nc.tensor.matmul(s_ps[:, k % 2, :], khh[:, b % 2, keys], q_hl[:, slot, :],
                                         start=True, stop=False)
                        nc.tensor.matmul(s_ps[:, k % 2, :], kly[0:DH + 2, b % 2, keys],
                                         q_hm[0:DH + 2, slot, :],
                                         start=False, stop=True).then_inc(score_mm, 1)
                    if kind == "PV":
                        pair, jt = divmod(a, JT)
                        k = u * UP + pair
                        pe.wait_ge(exp_done, k * 2 * JT + JT + jt + 1)
                        if a == 0:
                            pe.wait_ge(v_ready, b + 1)
                        if jt == 0 and k >= 1:
                            pe.wait_ge(raw_ready, k)
                        for hd in range(2):
                            head = 2 * k + hd
                            last = nc.tensor.matmul(pv_ps[DH * hd:DH * hd + DH, :], v[:, b % 2, jt, :],
                                                    prob[:, head % 4, jt, :], start=(jt == 0),
                                                    stop=(jt == JT - 1))
                        if jt == JT - 1:
                            last.then_inc(pv_mm, 1)
                    if kind == "SUM":
                        k = 2 * u + a
                        sums_done(pe, 4 * (k + 1))
                        if a == 0 and u >= 1:
                            pe.wait_ge(ao_ready, u * UP)
                        if a == 1 and u == last_unit:
                            pe.wait_ge(ao_ready, u * UP + 2)
                        for i in range(4):
                            last = nc.tensor.matmul(sum_ps[32 * i:32 * i + 32, :],
                                                    sumsel[:, 2 if u == last_unit else a, :],
                                                    psums[:, (4 * k + i) % SUM_SLOTS, :],
                                                    start=(a == 0 or u == last_unit),
                                                    stop=(a == 1 or u == last_unit), skip_group_check=True)
                        last.then_inc(sum_mm, 1)
                    if kind == "NORM":
                        k = u * UP + a
                        pe.wait_ge(recip_done, recips(u, a))
                        if k >= 1:
                            pe.wait_ge(ao_ready, k)
                        nc.tensor.matmul(sum_ps[:, :], headsel[:, a, :], rhl[:, :], start=True,
                                         stop=True).then_inc(norm_mm, 1)
                    if kind == "OUT":
                        k = u * UP + a
                        c = k % PAIRS
                        pe.wait_ge(ao_split, k + 1)
                        if c == 0 and b >= 1:
                            pe.wait_ge(y_ready, b)
                        product(y_ps[:, :], woh[:, c, :], wol[:, c, :], aoh[:, k % 2, :], aol[:, k % 2, :],
                                c == 0, c == PAIRS - 1).then_inc(out_mm, 1)
                    if kind in AFTER_STEPS:
                        after_tensor(pe, kind, u, q_ps)

        with ExitStack() as moe:
            for kept, name, shape in ((wguh, "wguh1", [P, 2 * F]), (wgul, "wgul1", [P, 2 * F]),
                                      (wdnh, "wdnh1", [P, FC, P]), (wdnl, "wdnl1", [P, FC, P])):
                kept.append(sb(moe, name, shape, F32R))
            xe = sb(moe, "xe", [P, 2, S])
            xeh = sb(moe, "xeh", [P, 2, S], F32R)
            xel = sb(moe, "xel", [P, 2, S], F32R)
            gl = sb(moe, "gl", [P, 2, S])
            ha = sb(moe, "ha", [P, 3, S])
            hh = sb(moe, "hh", [P, 4, S], F32R)
            hl = sb(moe, "hl", [P, 4, S], F32R)
            acc = sb(moe, "acc", [P, T])

            gate_ps = ps(moe, "gate_ps", [P, 2, S])
            up_ps = ps(moe, "up_ps", [P, 2, S])
            down_ps = ps(moe, "down_ps", [P, 2, S])
            turn_ps = [ps(moe, f"turn_ps{n}", [P, S]) for n in range(2)]
            bank = turn_ps[0]

            names = """xe_ready xeh_ready xel_ready gate_mm up_mm gelu_done ha_ready
                hh_ready hl_ready down_mm acc_done acc_turned out_ready out_sent""".split()
            (xe_ready, xeh_ready, xel_ready, gate_mm, up_mm, gelu_done, ha_ready,
             hh_ready, hl_ready, down_mm, acc_done, acc_turned, out_ready, out_sent) = [sem(n) for n in names]
            GROUPS = NB
            KS = E * GROUPS
            NS = KS * FC
            LB = NB - 1
            LAST_AFTER_AT = dict(zip(AFTER_STEPS, EXPERT_AFTER_AT))
            SPLIT_LAST_AT = 11
            SPLIT_WEIGHTS_AT = {6: 1, 26: 2}
            SPLIT_WEIGHTS_AT.update({((e - 1) * GROUPS + 1) * FC + 2: e for e in range(3, E)})
            DOWN_LAG = 3

            def scale_at(k):
                return k * FC - (2 if k == groups.index((0, LB)) else 6 if k >= 2 else 4)

            def after_steps(n):
                return [kind for kind in AFTER_STEPS if LAST_AFTER_AT[kind] == n]

            def down_done(eng, n):
                eng.wait_ge(down_mm, n + 1)

            block2 = moe.enter_context(nc.Block())

            @block2.sync
            def _(sp):
                def weights(e):
                    sp.wait_ge(w_split, 2 * (e - 1))
                    load_expert(sp, e)

                def combine(k):
                    sp.wait_ge(xe_ready, k - 3)
                    load_combine(sp, k)

                first_of_last = groups.index((0, LB))
                weights(2)
                for k in range(4, first_of_last):
                    combine(k)
                after_sync(sp, "ROWS", LB)
                sp.wait_ge(rows_out, 16 * NB)
                for k in range(first_of_last, KS):
                    combine(k)
                    if k % GROUPS == 0 and 3 <= k // GROUPS + 1 < E:
                        weights(k // GROUPS + 1)
                for b in range(NB):
                    sp.wait_ge(out_ready, b + 1)
                    sp.dma_start(out_t[b], x1[:, b * TPB:(b + 1) * TPB, :]).then_inc(out_sent, 16)
                sp.wait_ge(out_sent, 16 * NB)

            @block2.gpsimd
            def _(pool):
                def split_scaled(k):
                    pool.wait_ge(xe_ready, k + 1)
                    if k >= 2:
                        pool.wait_ge(up_mm, (k - 1) * FC)
                    nc.gpsimd.tensor_scalar(xeh[:, k % 2, :], xe[:, k % 2, :], 1.0, 1.0, ALU.mult,
                                            ALU.mult).then_inc(xeh_ready, 1)
                    pool.wait_ge(xeh_ready, k + 1)
                    nc.gpsimd.tensor_tensor(xel[:, k % 2, :], xe[:, k % 2, :], xeh[:, k % 2, :].bitcast(F32),
                                            ALU.subtract).then_inc(xel_ready, 1)

                split_scaled(0)
                for n in range(NS):
                    k, fc = divmod(n, FC)
                    for kind in after_steps(n):
                        after_gpsimd(pool, kind, LB)
                    if fc == 1 and k + 1 < KS:
                        split_scaled(k + 1)
                    e = SPLIT_WEIGHTS_AT.get(n)
                    if e is not None:
                        if e >= 2:
                            pool.wait_ge(down_mm, (groups.index((e - 2, LB)) + 1) * FC)
                        split_weights(pool, e)

            @block2.vector
            def _(dve):
                def scale_x(k):
                    e, g = groups[k]
                    dve.wait_ge(cb_in[k % 4], 16 * (k // 4 + 1))
                    if g == LB:
                        dve.wait_ge(x3T_ready, NB)
                    if k >= 2:
                        dve.wait_ge(xel_ready, k - 1)
                    nc.vector.tensor_tensor(xe[:, k % 2, :], x3T[:, g * S:(g + 1) * S], cb[:, k % 4, :],
                                            ALU.mult).then_inc(xe_ready, 1)

                def accumulate(k):
                    e, g = groups[k]
                    cols = slice(g * S, (g + 1) * S)
                    dve.wait_ge(down_mm, (k + 1) * FC)
                    if e == 0:
                        nc.vector.tensor_copy(acc[:, cols], down_ps[:, k % 2, :]).then_inc(acc_done, 1)
                    else:
                        dve.wait_ge(acc_done, groups.index((e - 1, g)) + 1)
                        nc.vector.tensor_tensor(acc[:, cols], acc[:, cols], down_ps[:, k % 2, :],
                                                ALU.add).then_inc(acc_done, 1)

                def low_part(n):
                    dve.wait_ge(hh_ready, n + 1)
                    nc.vector.tensor_tensor(hl[:, n % 4, :], ha[:, n % 3, :], hh[:, n % 4, :].bitcast(F32),
                                            ALU.subtract).then_inc(hl_ready, 1)

                def add_result(b):
                    tiles = x1[:, b * TPB:(b + 1) * TPB, :]
                    dve.wait_ge(acc_turned, b + 1)
                    nc.vector.tensor_tensor(tiles, tiles, turn_ps[b % 2][:, :].rearrange("p (t d) -> p t d", d=P),
                                            ALU.add).then_inc(out_ready, 1)

                scale_x(0)
                for n in range(NS):
                    k, fc = divmod(n, FC)
                    for kind in after_steps(n):
                        after_vector(dve, kind, LB, bank)
                    if n == SPLIT_LAST_AT:
                        x_low(dve, LB)
                    dve.wait_ge(gelu_done, n + 1)
                    dve.wait_ge(up_mm, n + 1)
                    if n >= 3:
                        dve.wait_ge(hl_ready, n - 2)
                    nc.vector.tensor_tensor(ha[:, n % 3, :], up_ps[:, n % 2, :], gl[:, n % 2, :],
                                            ALU.mult).then_inc(ha_ready, 1)
                    if n >= 1:
                        low_part(n - 1)
                    for later in range(1, KS):
                        if scale_at(later) == n:
                            scale_x(later)
                    if fc == 3 and k >= 1:
                        accumulate(k - 1)
                    if n in (NS - 5, NS - 1):
                        add_result((n - NS + 5) // 4)
                low_part(NS - 1)
                add_result(NB - 2)
                accumulate(KS - 1)
                add_result(NB - 1)
            @block2.scalar
            def _(act):
                def high_part(n):
                    act.wait_ge(ha_ready, n + 1)
                    if n >= 4:
                        down_done(act, n - 4)
                    nc.scalar.activation(hh[:, n % 4, :], ha[:, n % 3, :], ACT.Copy).then_inc(hh_ready, 1)

                for n in range(NS):
                    for kind in after_steps(n):
                        after_scalar(act, kind, LB, bank)
                    if n == SPLIT_LAST_AT:
                        act.wait_ge(x3T_ready, NB)
                        x_high(act, LB)
                    act.wait_ge(gate_mm, n + 1)
                    if n >= 2:
                        act.wait_ge(ha_ready, n - 1)
                    nc.scalar.activation(gl[:, n % 2, :], gate_ps[:, n % 2, :], ACT.Gelu).then_inc(gelu_done, 1)
                    if n >= 1:
                        high_part(n - 1)
                high_part(NS - 1)

            @block2.tensor
            def _(pe):
                def product(dst, wh, wl, mh, ml, start, stop):
                    nc.tensor.matmul(dst, wh, mh, start=start, stop=False)
                    nc.tensor.matmul(dst, wl, mh, start=False, stop=False)
                    return nc.tensor.matmul(dst, wh, ml, start=False, stop=stop)

                def down(n):
                    k, fc = divmod(n, FC)
                    e = groups[k][0]
                    pe.wait_ge(hl_ready, n + 1)
                    if fc == 0 and k >= 2:
                        pe.wait_ge(acc_done, k - 1)
                    product(down_ps[:, k % 2, :], wdnh[e % 2][:, fc, :], wdnl[e % 2][:, fc, :],
                            hh[:, n % 4, :], hl[:, n % 4, :], fc == 0, fc == FC - 1).then_inc(down_mm, 1)

                def turn_result(b):
                    pe.wait_ge(acc_done, (E - 1) * GROUPS + b + 1)
                    if b == 0:
                        pe.wait_ge(*after_bank_read(in_bank, LB))
                    if b >= 2:
                        pe.wait_ge(out_ready, b - 1)
                    for t in range(TPB):
                        last = nc.tensor.transpose(turn_ps[b % 2][:, t * P:(t + 1) * P],
                                                   acc[:, b * S + t * P:b * S + (t + 1) * P], ident[:, :])
                    last.then_inc(acc_turned, 1)

                in_bank = None
                for n in range(NS):
                    k, fc = divmod(n, FC)
                    e, g = groups[k]
                    cols = slice(g * S, (g + 1) * S)
                    for kind in after_steps(n):
                        if kind in ("YT", "X3T", "LOGIT", "ROWS"):
                            if in_bank:
                                pe.wait_ge(*after_bank_read(in_bank, LB))
                            in_bank = kind
                        after_tensor(pe, kind, LB, bank)
                    if g == 0 and fc == 0:
                        pe.wait_ge(w_split, 2 * (e + 1))
                    if e == 0 and fc == 0:
                        pe.wait_ge(x3l_ready, g + 1)
                    if n >= 2:
                        pe.wait_ge(gelu_done, n - 1)
                    fcols = slice(fc * P, (fc + 1) * P)
                    product(gate_ps[:, n % 2, :], wguh[e % 2][:, fcols], wgul[e % 2][:, fcols], x3h[:, cols],
                            x3l[:, cols], True, True).then_inc(gate_mm, 1)
                    if fc == 0:
                        pe.wait_ge(xel_ready, k + 1)
                    if n >= 2:
                        pe.wait_ge(ha_ready, n - 1)
                    ucols = slice(F + fc * P, F + (fc + 1) * P)
                    product(up_ps[:, n % 2, :], wguh[e % 2][:, ucols], wgul[e % 2][:, ucols], xeh[:, k % 2, :],
                            xel[:, k % 2, :], True, True).then_inc(up_mm, 1)
                    if n >= DOWN_LAG:
                        down(n - DOWN_LAG)
                    if n in (NS - 6, NS - 2):
                        turn_result((n - NS + 6) // 4)
                for n in range(NS - DOWN_LAG, NS):
                    if n == NS - 1:
                        turn_result(NB - 2)
                    down(n)
                turn_result(NB - 1)


def constants():
    import numpy as np

    eye = np.eye(P, dtype=np.float32)
    head_rows = np.zeros((P, UP, P), np.float32)
    for i in range(UH):
        for part in range(2):
            head_rows[32 * (i % 4) + i // 4 + 2 * part, i // 2, DH * (i % 2):DH * (i % 2) + DH] = 1.0
    low_parts = np.zeros((P, 1), np.float32)
    for quadrant in range(4):
        low_parts[32 * quadrant + 2:32 * quadrant + 4] = -1.0
    sum_rows = np.ones((P, 3, 32), np.float32)
    for rest in (0, 2):
        sum_rows[:, 0, 1 + rest] = 0.0
        sum_rows[:, 1, rest] = 0.0
    lower = np.ascontiguousarray(np.broadcast_to(np.tril(np.ones((8, 8), np.float32), -1), (P, 8, 8)))
    return {"eye": eye, "head_rows": head_rows, "sum_rows": sum_rows, "low_parts": low_parts,
            "lower": lower}


def kernel(**inputs):
    import numpy as _np
    import concourse.bacc as _bacc
    from concourse import mybir as _mybir
    from concourse.bass_utils import run_bass_kernel_spmd as _run

    def plain(name):
        return _np.ascontiguousarray(inputs[name])

    def turned(name, *axes):
        return _np.ascontiguousarray(_np.transpose(_np.asarray(inputs[name]), axes))

    data = {
        "x": plain("L0_attn_x"), "ln1_g": plain("L0_attn_ln1_g"), "ln1_b": plain("L0_attn_ln1_b"),
        "wq": plain("L0_attn_Wq"), "wkv": plain("L0_attn_Wkv"), "wo": plain("L0_attn_Wo"),
        "ln2_g": plain("L0_attn_ln2_g"), "ln2_b": plain("L0_attn_ln2_b"),
        "gate_wT": turned("L0_ffn_gate_w", 1, 0), "gate_upT": turned("L0_ffn_gate_up_w", 0, 2, 1),
        "downT": turned("L0_ffn_down_w", 0, 2, 1), **constants(),
    }
    nc = _bacc.Bacc("TRN2", target_bir_lowering=False, num_devices=1)
    arrays, args = {}, []
    for name, a in data.items():
        arrays[f"in_{name}"] = a
        args.append(nc.dram_tensor(f"in_{name}", a.shape, _mybir.dt.from_np(a.dtype), kind="ExternalInput").ap())
    out = nc.dram_tensor("out_0", data["x"].shape, F32, kind="ExternalOutput").ap()
    bass_preln_mqa_moe_kernel(nc, *args, out)
    r = _run(nc, [arrays], core_ids=[0])
    return r.results[0]["out_0"]
```
